# Optimizing a Trainium2 kernel written in Bass

```python
import numpy as np
import jax
import jax.numpy as jnp

def _softmax(x, axis=-1):
    return jax.nn.softmax(x, axis=axis)

def _gelu(x):
    return jax.nn.gelu(x, approximate=True)

def _silu(x):
    return jax.nn.silu(x)

def _sigmoid(x):
    return jax.nn.sigmoid(x)

def _layernorm(x, axis=-1, eps=1e-05):
    m = jnp.mean(x, axis=axis, keepdims=True)
    v = jnp.var(x, axis=axis, keepdims=True)
    return (x - m) / jnp.sqrt(v + eps)

def _scatter_add(tgt, idx, src, axis=0):
    return tgt.at[idx].add(src)

def _segment_sum(src, seg, n):
    return jax.ops.segment_sum(src, seg, n)
kernel_name = 'mk_vit_tower_cls_d1_tok_img512_r4_51b2c3'

def setup_inputs(seed: int=0):
    np.random.seed(seed)
    _w = jnp.asarray

    def _rec_inputs():
        import jax
        import jax.numpy as jnp
        _rk = jax.random.key(seed)
        x = -0.000356955 + 1 * jax.random.normal(jax.random.fold_in(_rk, 1), (64, 3, 96, 96), jnp.float32)
        cls_tok = 0.02 * jax.random.normal(jax.random.fold_in(_rk, 5), (1, 1, 128), jnp.float32)
        return (x, cls_tok)
    x, cls_tok = _rec_inputs()

    def _L0_tok_setup():
        import jax, jax.numpy as jnp
        import numpy as np
        key = jax.random.key(seed)
        k1, k2, k3 = jax.random.split(key, 3)
        B, C, H, W = (128, 3, 224, 224)
        E, p = (128, 16)
        K = C * p * p
        img = jax.random.normal(k1, (B, C, H, W), dtype=jnp.float32)
        w = jax.random.normal(k2, (E, K), dtype=jnp.float32) * (1.0 / np.sqrt(K))
        b = jax.random.normal(k3, (E,), dtype=jnp.float32)
        return {'img': img, 'w': w, 'b': b, 'patch_size': p}
    _L0_tok_all = _L0_tok_setup()
    _L0_tok_in = {k: v for k, v in _L0_tok_all.items() if k in ('w', 'b')}
    del _L0_tok_all

    def _L0_attn_setup():
        import jax, jax.numpy as jnp
        import numpy as np
        import math
        B, L, DIM, H = (2, 512, 128, 8)
        key = jax.random.key(seed)
        ks = jax.random.split(key, 8)
        s = 0.02
        return {'x': jax.random.normal(ks[0], (B, L, DIM), dtype=jnp.float32), 'Wq': jax.random.normal(ks[1], (DIM, DIM), dtype=jnp.float32) * s, 'Wk': jax.random.normal(ks[2], (DIM, DIM), dtype=jnp.float32) * s, 'Wv': jax.random.normal(ks[3], (DIM, DIM), dtype=jnp.float32) * s, 'Wb': jax.random.normal(ks[4], (H, DIM), dtype=jnp.float32) * s, 'mixing': jax.random.normal(ks[5], (H, DIM), dtype=jnp.float32) * 0.2, 'Wd': jax.random.normal(ks[6], (DIM, DIM), dtype=jnp.float32) * s, 'bd': jax.random.normal(ks[7], (DIM,), dtype=jnp.float32) * s}
    _L0_attn_all = _L0_attn_setup()
    _L0_attn_in = {k: v for k, v in _L0_attn_all.items() if k in ('Wq', 'Wk', 'Wv', 'Wb', 'mixing', 'Wd', 'bd')}
    del _L0_attn_all

    def _L0_ffn_setup():
        import jax, jax.numpy as jnp
        import numpy as np
        D_MODEL, N_GROUPS, N_EXPERTS = (128, 8, 8)
        TOP_K_L1, TOP_K_L2 = (2, 2)
        BATCH, SEQ = (2, 128)
        key = jax.random.key(seed)
        ks = jax.random.split(key, 6)
        d, G, E = (D_MODEL, N_GROUPS, N_EXPERTS)
        scale = 0.02
        x = jax.random.normal(ks[0], (BATCH, SEQ, d), dtype=jnp.float32)
        g1 = jax.random.normal(ks[1], (d, G), dtype=jnp.float32) * scale
        g2 = jax.random.normal(ks[2], (G, d, E), dtype=jnp.float32) * scale
        W1 = jax.random.normal(ks[3], (G, E, d, 2 * d), dtype=jnp.float32) * scale
        b1 = jnp.zeros((G, E, 2 * d), dtype=jnp.float32)
        W2 = jax.random.normal(ks[4], (G, E, 2 * d, d), dtype=jnp.float32) * scale
        b2 = jnp.zeros((G, E, d), dtype=jnp.float32)
        return {'x': x, 'g1': g1, 'g2': g2, 'W1': W1, 'b1': b1, 'W2': W2, 'b2': b2}
    _L0_ffn_all = _L0_ffn_setup()
    _L0_ffn_in = {k: v for k, v in _L0_ffn_all.items() if k in ('g1', 'g2', 'W1', 'b1', 'W2', 'b2')}
    del _L0_ffn_all
    return {'x': x, 'cls_tok': cls_tok, 'L0_tok_w': _L0_tok_in['w'], 'L0_tok_b': _L0_tok_in['b'], 'L0_attn_Wq': _L0_attn_in['Wq'], 'L0_attn_Wk': _L0_attn_in['Wk'], 'L0_attn_Wv': _L0_attn_in['Wv'], 'L0_attn_Wb': _L0_attn_in['Wb'], 'L0_attn_mixing': _L0_attn_in['mixing'], 'L0_attn_Wd': _L0_attn_in['Wd'], 'L0_attn_bd': _L0_attn_in['bd'], 'L0_ffn_g1': _L0_ffn_in['g1'], 'L0_ffn_g2': _L0_ffn_in['g2'], 'L0_ffn_W1': _L0_ffn_in['W1'], 'L0_ffn_b1': _L0_ffn_in['b1'], 'L0_ffn_W2': _L0_ffn_in['W2'], 'L0_ffn_b2': _L0_ffn_in['b2']}

def reference(x, cls_tok, L0_tok_w, L0_tok_b, L0_attn_Wq, L0_attn_Wk, L0_attn_Wv, L0_attn_Wb, L0_attn_mixing, L0_attn_Wd, L0_attn_bd, L0_ffn_g1, L0_ffn_g2, L0_ffn_W1, L0_ffn_b1, L0_ffn_W2, L0_ffn_b2):
    import jax
    import jax.numpy as jnp

    def _L0_tok_ref(img, w, b, patch_size):
        import jax, jax.numpy as jnp
        import numpy as np
        B, C, H, W = img.shape
        p = patch_size
        Hp, Wp = (H // p, W // p)
        S = Hp * Wp
        patches = img.reshape(B, C, Hp, p, Wp, p)
        patches = patches.transpose(0, 2, 4, 1, 3, 5).reshape(B, S, C * p * p)
        out = jnp.einsum('bsk,ek->bse', patches, w) + b
        return out

    def _L0_attn_ref(x, Wq, Wk, Wv, Wb, mixing, Wd, bd):
        import jax, jax.numpy as jnp
        import numpy as np
        import math
        B, L, DIM, H = (2, 512, 128, 8)
        b, l, d = x.shape
        h = mixing.shape[0]
        dh = d // h
        q = x @ Wq.T
        k = x @ Wk.T
        v = (x @ Wv.T).reshape(b, l, h, dh).transpose(0, 2, 1, 3)
        scores = jnp.einsum('bld,hd,bsd->bhls', q, mixing, k)
        cb = jnp.einsum('bsd,hd->bhs', x, Wb)
        scale = math.sqrt(d / h)
        scores = (scores + cb[:, :, None, :]) / scale
        probs = jax.nn.softmax(scores, axis=-1)
        ctx = jnp.einsum('bhls,bhsd->bhld', probs, v)
        ctx = ctx.transpose(0, 2, 1, 3).reshape(b, l, d)
        return ctx @ Wd.T + bd

    def _L0_ffn_ref(x, g1, g2, W1, b1, W2, b2):
        import jax, jax.numpy as jnp
        import numpy as np
        D_MODEL, N_GROUPS, N_EXPERTS = (128, 8, 8)
        TOP_K_L1, TOP_K_L2 = (2, 2)
        BATCH, SEQ = (2, 128)
        B, S, d = x.shape
        G, E = (g1.shape[1], g2.shape[2])
        xt = x.reshape(-1, d)
        logits1 = xt @ g1
        v1, i1 = jax.lax.top_k(logits1, TOP_K_L1)
        w1 = jax.nn.softmax(v1.astype(jnp.float32), axis=-1).astype(x.dtype)
        c1 = jnp.sum(jax.nn.one_hot(i1, G, dtype=x.dtype) * w1[..., None], axis=1)
        logits2 = jnp.einsum('td,gde->tge', xt, g2)
        v2, i2 = jax.lax.top_k(logits2, TOP_K_L2)
        w2 = jax.nn.softmax(v2.astype(jnp.float32), axis=-1).astype(x.dtype)
        c2 = jnp.sum(jax.nn.one_hot(i2, E, dtype=x.dtype) * w2[..., None], axis=2)
        h = jax.nn.relu(jnp.einsum('td,gedh->tgeh', xt, W1) + b1)
        y = jnp.einsum('tgeh,gehd->tged', h, W2) + b2
        group_out = jnp.einsum('tged,tge->tgd', y, c2)
        out = jnp.einsum('tgd,tg->td', group_out, c1)
        return out.reshape(B, S, d)
    h = _L0_tok_ref(x, L0_tok_w, L0_tok_b, 16)
    h = jnp.concatenate([jnp.broadcast_to(cls_tok, (h.shape[0], 1, h.shape[2])), h], axis=1)
    h = h + _L0_attn_ref(_layernorm(h, axis=-1), L0_attn_Wq, L0_attn_Wk, L0_attn_Wv, L0_attn_Wb, L0_attn_mixing, L0_attn_Wd, L0_attn_bd)
    h = h + _L0_ffn_ref(_layernorm(h, axis=-1), L0_ffn_g1, L0_ffn_g2, L0_ffn_W1, L0_ffn_b1, L0_ffn_W2, L0_ffn_b2)
    return h

_drawn_inputs = setup_inputs


def setup_inputs(seed=0):
    import zlib

    import numpy as np

    out = dict(_drawn_inputs(seed))
    spreads = {'L0_ffn_b1': (0.0, 0.8), 'L0_ffn_b2': (0.0, 0.1)}
    factors = {'cls_tok': 8.0,
     'L0_attn_Wq': 8.0,
     'L0_attn_Wk': 8.0,
     'L0_attn_Wb': 34.749,
     'L0_attn_mixing': 8.0,
     'L0_attn_bd': 3.27,
     'L0_ffn_W1': 3.643,
     'L0_ffn_W2': 2.752}
    for name, (base, spread) in spreads.items():
        noise = np.random.default_rng([zlib.crc32(name.encode()), seed]).standard_normal(out[name].shape)
        drawn = base * np.exp(spread * noise) if base else spread * noise
        out[name] = jnp.asarray(drawn.astype(out[name].dtype))
    for name, factor in factors.items():
        out[name] = (out[name] * factor).astype(out[name].dtype)
    return out
```

```python
from contextlib import ExitStack

import concourse.bass as bass
from concourse import mybir

P = 128
IMAGES = 64
PATCHES = 36
TOK = PATCHES + 1
D = 128
K_CHUNKS = 3 * 16 * 16 // P
HEADS = 8
DH = D // HEADS
T = IMAGES * TOK
TILES = -(-T // P)
TP = TILES * P
LAST = T - (TILES - 1) * P
GROUP = 8
GROUPS_OF_IMAGES = IMAGES // GROUP
GP = GROUP * PATCHES
GT = GROUP * TOK
PAIRS = IMAGES // 2
PT = 2 * TOK
HS = HEADS * TOK
NG = 8
NE = 8
EXPERTS = NG * NE
HID = 2 * D
PICKS = 4
EXPERT_TILES = T * PICKS // P + EXPERTS
SLOTS = EXPERT_TILES * P
RING = 6
SPLITS = 3
EPS = 1e-5
SCALE = (D / HEADS) ** -0.5
MID = T // 2
LOW = -3.0e38

C_TOKW = 0
C_Q = C_TOKW + K_CHUNKS * P
C_K = C_Q + D
C_V = C_K + D
C_D = C_V + D
C_R = C_D + D
C_B = C_R + NG + EXPERTS
C_MIX = C_B + HEADS
C_B1 = C_MIX + HEADS
C_TOKB = C_B1 + 2 * EXPERTS
C_CLS = C_TOKB + 1
C_BD = C_CLS + 1
C_ALL = C_BD + 1

ALU = mybir.AluOpType
ACT = mybir.ActivationFunctionType
AX = mybir.AxisListType
F32 = mybir.dt.float32
BF16 = mybir.dt.bfloat16
FP16 = mybir.dt.float16
I32 = mybir.dt.int32
ds = bass.ds


def build(nc, patches, small, w1_dram, w2_dram, b2_dram, out):
    assert T * PICKS % P == 0 and EXPERT_TILES % RING == 0 and PAIRS % 2 == 0 and GROUPS_OF_IMAGES % 2 == 0
    with ExitStack() as ctx:
        def sb(name, shape, dt=F32):
            return ctx.enter_context(nc.sbuf_tensor(name, shape, dt))

        def sem(name):
            return ctx.enter_context(nc.semaphore(name))

        bank = [ctx.enter_context(nc.psum_tensor(f"bank{i}", [P, 512], F32)) for i in range(8)]

        bias_dram = nc.dram_tensor("bias_dram", [SPLITS, HEADS, T], BF16, kind="Internal").ap()
        xn_dram = nc.dram_tensor("xn_dram", [TP, D], F32, kind="Internal").ap()
        y_dram = nc.dram_tensor("y_dram", [SLOTS, D], F32, kind="Internal").ap()

        w1 = sb("w1", [P, EXPERTS * HID])
        w2 = sb("w2", [P, EXPERTS * HID])
        b2 = sb("b2", [EXPERTS, D])
        wp = sb("wp", [P, C_ALL])
        ident = sb("ident", [P, P])
        center = sb("center", [P, P])
        average = sb("average", [P, P])
        earlier = sb("earlier", [P, P], BF16)
        ones_b = sb("ones_b", [P, P], BF16)
        ones_f = sb("ones_f", [P, EXPERTS])
        eps = sb("eps", [P, 1])
        iota8 = sb("iota8", [P, NE])
        iota_slot = sb("iota_slot", [P, P], FP16)
        iota_tile = sb("iota_tile", [P, EXPERT_TILES], FP16)
        tile_no = sb("tile_no", [P, 2])
        tok_val = sb("tok_val", [P, TILES])
        hT = sb("hT", [P, TP])

        arena_words = 14400
        arena = sb("arena", [P, arena_words])
        used = [0]

        def at(shape, dt=F32):
            n = 1
            for s in shape[1:]:
                n *= s
            words = n if dt in (F32, I32) else -(-n // 2)
            a = arena[0:shape[0], used[0]:used[0] + words]
            used[0] += words
            assert used[0] <= arena_words, used[0]
            if dt != F32:
                a = a.bitcast(dt)
            if len(shape) > 2:
                names = "abcd"[:len(shape) - 1]
                a = a.rearrange("p (" + " ".join(names) + ") -> p " + " ".join(names),
                                **{k: s for k, s in zip(names, shape[1:])})
            return a

        xnT = at([P, T])
        qT = at([P, TP])
        kT = at([P, T])
        used_ab = used[0]
        x_sb = w2[:, 0:K_CHUNKS * GP * GROUPS_OF_IMAGES].rearrange("p (g c n) -> p g c n", c=K_CHUNKS, n=GP)
        bias_parts = w1[0:HEADS, 0:SPLITS * T // 2].bitcast(BF16).rearrange("p (s t) -> p s t", s=SPLITS)
        squares = at([P, GT])
        spread = at([P, GT])
        inv = at([P, GT])
        cb_f = at([HEADS, GT])
        cb_r = at([HEADS, GT])
        cb_m = at([HEADS, GT])
        used[0] = used_ab
        xs = at([P, 2, 2, P])
        qs = at([P, 2, 2, 64])
        km = at([P, 2, 2, HS])
        bias_row = at([SPLITS, 2, HEADS * PT], BF16)
        v_sb = at([P, 2, 2, D])
        e_sb = at([P, 2, HEADS, 64])
        top = at([P, 2, HEADS])
        total = at([P, 2, HEADS])
        inv_total = at([P, 2, HEADS])
        used_b = used[0]

        pT = sb("pT", [P, 2, HEADS // 2, 2, TOK])
        ctx_sb = sb("ctx_sb", [P, D])
        ctxT = sb("ctxT", [P, PT])

        used[0] = 0
        h_tok = at([P, TILES, D])
        logits = at([P, TILES, NG + EXPERTS])
        base_e = at([P, EXPERTS])
        c_all = at([P, TILES, EXPERTS])
        weight = at([P, TILES, PICKS])
        pos_i = at([P, TILES, PICKS], I32)
        slot_token = at([P, EXPERT_TILES], I32)
        tile_expert = at([1, 2 * P], I32)
        used_c = used[0]
        stats = at([P, TILES, 6])
        mean2 = at([P, TILES])
        var2 = at([P, TILES])
        diff2 = at([P, TILES])
        sd2 = at([P, TILES])
        rstd2 = at([P, TILES])
        hs = at([P, 2, P])
        xn_row = at([P, 2, D])
        xnT2 = at([P, 2, P])
        used[0] = used_c
        prod = at([P, TILES, NG, NE])
        seen = at([P, TILES + 1, EXPERTS], BF16)
        oh1 = [at([P, TILES, NG]) for _ in range(2)]
        sel = at([P, TILES, 2, NE])
        oh2 = [at([P, TILES, 2, NE]) for _ in range(2)]
        tmp_x = at([P, TILES, 2, NE])
        tmp_i = at([P, TILES, 2, NE])
        best = at([P, 2, 2, TILES * 2])
        lowest = at([P, TILES * 2])
        gap = at([P, 2, TILES * 2])
        egap = at([P, 2, TILES * 2])
        den = at([P, 2, TILES * 2])
        share = at([P, 2, 2, TILES * 2])
        count_i = at([P, EXPERTS], I32)
        count_s = at([P, EXPERTS], I32)
        tiles_f = at([P, EXPERTS])
        tiles_end = at([P, EXPERTS])
        cmp = at([P, EXPERTS])
        e_col = at([P, 2])
        pos_f = at([P, TILES, PICKS])
        hi_i = at([P, TILES, PICKS], I32)
        hi_f = at([P, TILES, PICKS])
        lo_f = at([P, TILES, PICKS])
        onehot_slot = at([P, PICKS, P], FP16)
        onehot_tile = at([P, PICKS, EXPERT_TILES], FP16)
        used[0] = used_c
        idx_now = at([P, RING], I32)
        xg = at([P, RING, D])
        xgT = at([P, 2, P])
        hid = at([P, 2, HID])
        hidT = at([P, 2, 2, P])
        y_sb = at([P, RING, D])
        used[0] = used_c
        pos_now = at([P, 2, PICKS], I32)
        y_got = at([P, 2, PICKS, D])
        c_now = at([P, 2, 2, EXPERTS])
        cT = at([EXPERTS, 2, P])
        acc = at([P, 2, D])

        S = {n: sem(n) for n in """
            small_loaded b2_loaded w1_loaded w2_loaded bias_stored xn_stored_a xn_stored_b out_stored_a out_stored_b
            x_loaded_a x_loaded_b bias_loaded_a bias_loaded_b
            identity_made consts_made pool_step cls_placed
            embed_mm h_placed center_mm squared var_mm spread_done inv_done xn_done qk_mm q_done k_done bias_split split_step
            xs_copied qs_copied km_done score_mm v_mm v_done maxed lessened exped summed inverted probs_done
            probs_turned pT_done context_mm ctx_copied context_turned ctxT_done project_mm h_added pads_done
            hs_copied h_turned h_rowed stat_done var_step var_ready spread2_done inv2_done xn_rowed xn_turned xnT_done logit_mm logit_done
            route gap_ready exp_ready mask_ready rank_mm c_ready share_ready step_c ecol_ready erow_mm tiles_known
            onehot_done table_mm table_done rank_read
            idx_copied x_turned xT_done hidden_mm hidden_done hidden_turned relu_done y_mm y_done
            pos_copied c_copied c_turned cT_done b2_mm base_done acc_step acc_done""".split()}
        gathered = [sem(f"gathered{r}") for r in range(RING)]
        y_stored = [sem(f"y_stored{r}") for r in range(RING)]
        y_fetched = [sem(f"y_fetched{r}") for r in range(2)]
        x_loaded = [S["x_loaded_a"], S["x_loaded_b"]]
        bias_loaded = [S["bias_loaded_a"], S["bias_loaded_b"]]
        xn_stored = [S["xn_stored_a"], S["xn_stored_b"]]
        out_stored = [S["out_stored_a"], S["out_stored_b"]]

        def steps(eng, n, lag, step, ahead=0):
            first = (lag + 3) // 2 * 2
            last = n - ahead - (n - ahead - first) % 2
            for i in range(first):
                step(i, i % 2, i, n)
            if last > first:
                with_loop(eng, first, last, 2, lambda i: (step(i, 0, None, n), step(i + 1, 1, None, n)))
            for i in range(last, n + lag):
                step(i, i % 2, i, n)

        def with_loop(eng, a, b, stride, body):
            with eng.Fori(a // stride, b // stride, 1) as n:
                body(n * stride)

        def live(known, lag, n):
            return known is None or 0 <= known - lag < n

        def past(known, m):
            return known is None or known >= m

        block = ctx.enter_context(nc.Block())

        @block.sync
        def _(sp):
            sp.dma_start(wp[:, :], small).then_inc(S["small_loaded"], 16)
            for g in range(2):
                sp.dma_start(x_sb[:, g], patches[g]).then_inc(x_loaded[g], 16)
            with sp.Fori(1, GROUPS_OF_IMAGES // 2, 1) as turn:
                g = turn * 2
                for r in range(2):
                    sp.wait_ge(x_loaded[r], g * 8)
                    sp.dma_start(x_sb[:, ds(g + r, 1)], patches[ds(g + r, 1)].rearrange("g p c n -> p g c n")
                                 ).then_inc(x_loaded[r], 16)
            sp.dma_start(b2[:, :], b2_dram).then_inc(S["b2_loaded"], 16)
            sp.wait_ge(S["bias_split"], GROUPS_OF_IMAGES)
            for s in range(SPLITS):
                sp.dma_start(bias_dram[s], bias_parts[:, s]).then_inc(S["bias_stored"], 16)
            sp.wait_ge(S["bias_stored"], 16 * SPLITS)
            for r in range(2):
                sp.dma_start(bias_row[:, r].rearrange("s (h t) -> s h t", h=HEADS),
                             bias_dram[:, :, r * PT:(r + 1) * PT]).then_inc(bias_loaded[r], 16)
            sp.dma_start(w1[:, :], w1_dram).then_inc(S["w1_loaded"], 16)
            sp.dma_start(w2[:, :], w2_dram).then_inc(S["w2_loaded"], 16)
            with sp.Fori(1, PAIRS // 2, 1) as turn:
                p = turn * 2
                for r in range(2):
                    sp.wait_ge(S["score_mm"], p + r - 1)
                    sp.dma_start(bias_row[:, r].rearrange("s (h t) -> s h t", h=HEADS),
                                 bias_dram[:, :, ds((p + r) * PT, PT)]).then_inc(bias_loaded[r], 16)
            def store_xn(i, r):
                sp.wait_ge(S["xn_rowed"], i + 1)
                sp.dma_start(xn_dram[ds(i * P, P)], xn_row[:, r]).then_inc(xn_stored[r], 16)
            with sp.Fori(0, (TILES - 1) // 2, 1) as turn:
                i = turn * 2
                store_xn(i, 0)
                store_xn(i + 1, 1)
            store_xn(TILES - 1, 0)
            with sp.Fori(0, EXPERT_TILES // RING, 1) as turn:
                j = turn * RING
                for r in range(RING):
                    sp.wait_ge(S["y_done"], j + r + 1)
                    sp.dma_start(y_dram[ds((j + r) * P, P)], y_sb[:, r]).then_inc(y_stored[r], 16)
            rows = out.rearrange("b s d -> (b s) d")
            with sp.Fori(0, (TILES - 1) // 2, 1) as turn:
                i = turn * 2
                for r in range(2):
                    sp.wait_ge(S["acc_done"], i + r + 1)
                    sp.dma_start(rows[ds((i + r) * P, P)], acc[:, r]).then_inc(out_stored[r], 16)
            sp.wait_ge(S["acc_done"], TILES)
            sp.dma_start(rows[(TILES - 1) * P:T], acc[0:LAST, 0]).then_inc(out_stored[0], 16)
            sp.wait_ge(out_stored[0], 16 * (TILES // 2 + 1))
            sp.wait_ge(out_stored[1], 16 * (TILES // 2))

        @block.gpsimd
        def _(pool):
            g = nc.gpsimd
            g.memset(ident[:, :], 0.0)
            g.memset(earlier[:, :], 1.0)
            g.memset(tok_val[:, :], 0.0)
            g.memset(average[:, :], 1.0 / D).then_inc(S["pool_step"], 1)
            pool.wait_ge(S["pool_step"], 1)
            g.affine_select(out=ident[:, :], in_=ident[:, :], compare_op=ALU.not_equal, fill=1.0, base=0,
                            pattern=[[-1, P]], channel_multiplier=1).then_inc(S["pool_step"], 1)
            g.affine_select(out=earlier[:, :], in_=earlier[:, :], compare_op=ALU.is_gt, fill=0.0, base=0,
                            pattern=[[1, P]], channel_multiplier=-1)
            pool.wait_ge(S["pool_step"], 2)
            g.tensor_scalar(center[:, :], ident[:, :], 1.0 / D, None, ALU.subtract)
            g.memset(ones_b[:, :], 1.0)
            g.memset(ones_f[:, :], 1.0)
            g.memset(ctx_sb[:, :], 0.0)
            g.memset(eps[:, :], EPS)
            g.iota(iota8[:, :], pattern=[[1, NE]], base=0, channel_multiplier=0, allow_small_or_imprecise_dtypes=True)
            g.iota(iota_slot[:, :], pattern=[[1, P]], base=0, channel_multiplier=0, allow_small_or_imprecise_dtypes=True)
            g.iota(iota_tile[:, :], pattern=[[1, EXPERT_TILES]], base=0, channel_multiplier=0,
                   allow_small_or_imprecise_dtypes=True)
            g.iota(tile_no[:, :], pattern=[[P, 2]], base=0, channel_multiplier=1, allow_small_or_imprecise_dtypes=True)
            g.iota(tok_val[:, 0:TILES - 1], pattern=[[P, TILES - 1]], base=-MID, channel_multiplier=1,
                   allow_small_or_imprecise_dtypes=True)
            g.iota(tok_val[0:LAST, TILES - 1:TILES], pattern=[[P, 1]], base=(TILES - 1) * P - MID, channel_multiplier=1,
                   allow_small_or_imprecise_dtypes=True).then_inc(S["consts_made"], 1)

            mix = wp[:, C_MIX:C_MIX + HEADS].unsqueeze(2).to_broadcast([P, HEADS, TOK])

            def attend(p, r, known, n):
                if live(known, 0, n):
                    if known == 0:
                        pool.wait_ge(S["k_done"], GROUPS_OF_IMAGES)
                        pool.wait_ge(S["bias_split"], GROUPS_OF_IMAGES)
                    if past(known, 2):
                        pool.wait_ge(S["score_mm"], p - 1)
                    for a in range(2):
                        last = g.tensor_tensor(
                            km[:, r, a].rearrange("p (h s) -> p h s", h=HEADS),
                            kT[:, ds(p * PT + a * TOK, TOK)].unsqueeze(1).to_broadcast([P, HEADS, TOK]), mix, ALU.mult)
                    last.then_inc(S["km_done"], 1)
                if live(known, 1, n):
                    pool.wait_ge(S["inverted"], p)
                    e = e_sb[:, 1 - r, :, 0:TOK]
                    g.tensor_tensor(e, e, inv_total[:, 1 - r].unsqueeze(2).to_broadcast([P, HEADS, TOK]), ALU.mult
                                    ).then_inc(S["probs_done"], 1)
            steps(pool, PAIRS, 1, attend)

            pool.wait_ge(S["share_ready"], 1)
            n_c = [0]

            def link(ins):
                n_c[0] += 1
                ins.then_inc(S["step_c"], 1)
                pool.wait_ge(S["step_c"], n_c[0])

            def bc(a, shape):
                return a.to_broadcast(shape)

            sh2 = [share[:, 1, b, :].rearrange("p (i a) -> p i a", a=2).unsqueeze(3) for b in range(2)]
            link(g.tensor_tensor(sel, oh2[0], bc(sh2[0], [P, TILES, 2, NE]), ALU.mult))
            link(g.tensor_tensor(tmp_x, oh2[1], bc(sh2[1], [P, TILES, 2, NE]), ALU.mult))
            link(g.tensor_tensor(sel, sel, tmp_x, ALU.add))
            for a in range(2):
                sh1 = share[:, 0, a, 0:TILES].unsqueeze(2)
                link(g.tensor_tensor(sel[:, :, a], sel[:, :, a], bc(sh1, [P, TILES, NE]), ALU.mult))
            call = c_all.rearrange("p i (g e) -> p i g e", g=NG)
            link(g.tensor_tensor(call, bc(oh1[0].unsqueeze(3), [P, TILES, NG, NE]),
                                 bc(sel[:, :, 0].unsqueeze(2), [P, TILES, NG, NE]), ALU.mult))
            pool.wait_ge(S["rank_read"], 1)
            link(g.tensor_tensor(prod, bc(oh1[1].unsqueeze(3), [P, TILES, NG, NE]),
                                 bc(sel[:, :, 1].unsqueeze(2), [P, TILES, NG, NE]), ALU.mult))
            g.tensor_tensor(call, call, prod, ALU.add).then_inc(S["c_ready"], 1)

            for r in range(2):
                pool.wait_ge(xn_stored[r], 16 * ((TILES + 1 - r) // 2))

            def gather(j, r, again):
                copied = j + r + 1 if not again else pool.to_reg(j + r + 1)
                pool.wait_ge(S["table_done"], 1)
                pool.wait_ge(S["idx_copied"], copied)
                g.indirect_dma_start(xg[:, r], None, xn_dram, bass.IndirectOffsetOnAxis(idx_now[:, r:r + 1], 0)
                                     ).then_inc(gathered[r], 16)
            for r in range(RING):
                gather(0, r, False)
            with pool.Fori(1, EXPERT_TILES // RING, 1) as turn:
                j = turn * RING
                for r in range(RING):
                    gather(j, r, True)

            for r in range(RING):
                pool.wait_ge(y_stored[r], 16 * (EXPERT_TILES // RING))

            def fetch(i, r, again):
                copied = i + 1 if not again else pool.to_reg(i + 1)
                pool.wait_ge(S["table_done"], 1)
                pool.wait_ge(S["pos_copied"], copied)
                for k in range(PICKS):
                    g.indirect_dma_start(y_got[:, r, k], None, y_dram,
                                         bass.IndirectOffsetOnAxis(pos_now[:, r, k:k + 1], 0)).then_inc(y_fetched[r], 16)
            fetch(0, 0, False)
            fetch(1, 1, False)
            with pool.Fori(1, (TILES - 1) // 2, 1) as turn:
                i = turn * 2
                fetch(i, 0, True)
                fetch(i + 1, 1, True)
            fetch(TILES - 1, 0, True)

        @block.scalar
        def _(act):
            s = nc.scalar
            act.wait_ge(S["small_loaded"], 16)
            act.wait_ge(S["consts_made"], 1)

            def embed(i, r, known, n):
                if live(known, 0, n):
                    act.wait_ge(S["embed_mm"], i + 1)
                    s.activation(hT[:, ds(i * GT, GT)].rearrange("p (b t) -> p b t", t=TOK)[:, :, 1:TOK],
                                 bank[0][:, 0:GP].rearrange("p (b t) -> p b t", t=PATCHES), ACT.Identity,
                                 bias=wp[:, C_TOKB:C_TOKB + 1]).then_inc(S["h_placed"], 1)
                if live(known, 1, n):
                    act.wait_ge(S["var_mm"], i)
                    if past(known, 2):
                        act.wait_ge(S["inv_done"], i - 1)
                    s.activation(spread, bank[3][:, 0:GT], ACT.Sqrt, bias=eps[:, :]).then_inc(S["spread_done"], 1)
                if live(known, 2, n):
                    act.wait_ge(S["qk_mm"], i - 1)
                    s.activation(qT[:, ds((i - 2) * GT, GT)], bank[4][:, 0:GT], ACT.Copy, scale=SCALE
                                 ).then_inc(S["q_done"], 1)
                if live(known, 0, n):
                    act.wait_ge(S["center_mm"], i + 1)
                    s.activation(squares, bank[1 + r][:, 0:GT], ACT.Square).then_inc(S["squared"], 1)
            steps(act, GROUPS_OF_IMAGES, 2, embed)

            def attend(p, r, known, n):
                if live(known, 0, n):
                    act.wait_ge(S["lessened"], p + 1)
                    s.activation(e_sb[:, r, :, 0:TOK], e_sb[:, r, :, 0:TOK], ACT.Exp).then_inc(S["exped"], 1)
                if live(known, 1, n):
                    act.wait_ge(S["v_mm"], p)
                    if past(known, 3):
                        act.wait_ge(S["context_mm"], p - 2)
                    s.activation(v_sb[:, 1 - r], bank[2][:, 0:2 * D].rearrange("p (a d) -> p a d", a=2), ACT.Copy
                                 ).then_inc(S["v_done"], 1)
                    act.wait_ge(S["probs_turned"], p)
                    s.activation(pT[:, 1 - r],
                                 bank[3][:, :].rearrange("p (h a t) -> p h a t", h=4, a=2)[:, :, :, 0:TOK],
                                 ACT.Copy).then_inc(S["pT_done"], 1)
                if live(known, 3, n):
                    act.wait_ge(S["context_turned"], p - 2)
                    if past(known, 4):
                        act.wait_ge(S["project_mm"], p - 3)
                    s.activation(ctxT[:, :].rearrange("p (a t) -> p a t", a=2),
                                 bank[6][:, 0:P].rearrange("p (a t) -> p a t", a=2)[:, :, 0:TOK], ACT.Copy
                                 ).then_inc(S["ctxT_done"], 1)
            steps(act, PAIRS, 3, attend)

            act.wait_ge(S["h_added"], PAIRS)

            def rows_of_h(i, r, known, n):
                act.wait_ge(S["h_turned"], i + 1)
                s.activation(h_tok[:, ds(i, 1)].rearrange("p i d -> p (i d)"), bank[r][:, 0:P], ACT.Copy
                             ).then_inc(S["h_rowed"], 1)
            steps(act, TILES, 0, rows_of_h)
            act.wait_ge(S["var_ready"], 1)
            s.activation(sd2, var2, ACT.Sqrt, bias=eps[:, :]).then_inc(S["spread2_done"], 1)

            def rows_of_xn(i, r, known, n):
                act.wait_ge(S["xn_turned"], i + 1)
                if past(known, 2):
                    act.wait_ge(S["logit_mm"], i - 1)
                s.activation(xnT2[:, r], bank[2 + r][:, 0:P], ACT.Copy).then_inc(S["xnT_done"], 1)
            steps(act, TILES, 0, rows_of_xn)

            act.wait_ge(S["gap_ready"], 1)
            s.activation(egap, gap, ACT.Exp).then_inc(S["exp_ready"], 1)

            act.wait_ge(S["tiles_known"], 1)

            def expert(j, r, known, n):
                if live(known, 0, n):
                    act.wait_ge(S["x_turned"], j + 1)
                    if past(known, 2):
                        act.wait_ge(S["hidden_mm"], j - 1)
                    s.activation(xgT[:, r], bank[r][:, 0:P], ACT.Copy).then_inc(S["xT_done"], 1)
                if live(known, 2, n):
                    e = act.value_load(tile_expert[0:1, ds(j - 2, 1)], min_val=0, max_val=EXPERTS - 1)
                    act.wait_ge(S["hidden_turned"], j - 1)
                    if past(known, 4):
                        act.wait_ge(S["y_mm"], j - 3)
                    for half in range(2):
                        last = s.activation(hidT[:, r, half], bank[4 + r][:, half * P:half * P + P], ACT.Relu,
                                            bias=wp[:, ds(C_B1 + 2 * e + half, 1)])
                    last.then_inc(S["relu_done"], 1)
            steps(act, EXPERT_TILES, 2, expert)

            act.wait_ge(S["c_ready"], 1)
            for r in range(RING):
                act.wait_ge(y_stored[r], 16 * (EXPERT_TILES // RING))

            def biases(i, r, known, n):
                if live(known, 0, n):
                    if past(known, 2):
                        act.wait_ge(S["c_turned"], i - 1)
                    s.activation(c_now[:, r], c_all[:, ds(i, 1)].to_broadcast([P, 2, EXPERTS]), ACT.Copy
                                 ).then_inc(S["c_copied"], 1)
                    act.wait_ge(S["c_turned"], i + 1)
                    if past(known, 2):
                        act.wait_ge(S["b2_mm"], i - 1)
                    s.activation(cT[:, r], bank[r][0:EXPERTS, 0:P], ACT.Copy).then_inc(S["cT_done"], 1)
            steps(act, TILES, 0, biases)

        @block.tensor
        def _(pe):
            t = nc.tensor
            pe.wait_ge(S["small_loaded"], 16)
            pe.wait_ge(S["consts_made"], 1)

            def embed(i, r, known, n):
                if live(known, 0, n):
                    pe.wait_ge(x_loaded[r], (i - r) * 8 + 16)
                    if past(known, 1):
                        pe.wait_ge(S["h_placed"], i)
                    for c in range(K_CHUNKS):
                        last = t.matmul(bank[0][:, 0:GP], wp[:, C_TOKW + c * P:C_TOKW + (c + 1) * P],
                                        x_sb[:, ds(i, 1), c].rearrange("p g n -> p (g n)"),
                                        start=(c == 0), stop=(c == K_CHUNKS - 1))
                    last.then_inc(S["embed_mm"], 1)
                if live(known, 1, n):
                    pe.wait_ge(S["squared"], i)
                    if past(known, 2):
                        pe.wait_ge(S["spread_done"], i - 1)
                    t.matmul(bank[3][:, 0:GT], average[:, :], squares, start=True, stop=True).then_inc(S["var_mm"], 1)
                if live(known, 2, n):
                    pe.wait_ge(S["xn_done"], i - 1)
                    if past(known, 3):
                        pe.wait_ge(S["q_done"], i - 2)
                        pe.wait_ge(S["k_done"], i - 2)
                        pe.wait_ge(S["bias_split"], i - 2)
                    xg_ = xnT[:, ds((i - 2) * GT, GT)]
                    t.matmul(bank[4][:, 0:GT], wp[:, C_Q:C_Q + D], xg_, start=True, stop=True)
                    t.matmul(bank[5][:, 0:GT], wp[:, C_K:C_K + D], xg_, start=True, stop=True)
                    t.matmul(bank[6][0:HEADS, 0:GT], wp[:, C_B:C_B + HEADS], xg_, start=True, stop=True
                             ).then_inc(S["qk_mm"], 1)
                if live(known, 0, n):
                    pe.wait_ge(S["h_placed"], i + 1)
                    if past(known, 2):
                        pe.wait_ge(S["xn_done"], i - 1)
                    else:
                        pe.wait_ge(S["cls_placed"], 1)
                    t.matmul(bank[1 + r][:, 0:GT], center[:, :], hT[:, ds(i * GT, GT)], start=True, stop=True
                             ).then_inc(S["center_mm"], 1)
            steps(pe, GROUPS_OF_IMAGES, 2, embed)
            pe.wait_ge(S["q_done"], GROUPS_OF_IMAGES)
            pe.wait_ge(S["k_done"], GROUPS_OF_IMAGES)

            def attend(p, r, known, n):
                if live(known, 0, n):
                    pe.wait_ge(S["qs_copied"], p + 1)
                    pe.wait_ge(S["km_done"], p + 1)
                    pe.wait_ge(bias_loaded[r], (p - r) * 8 + 16)
                    if past(known, 2):
                        pe.wait_ge(S["lessened"], p - 1)
                    for a in range(2):
                        scores = bank[r][64 * a:64 * a + 64, 0:HS]
                        t.matmul(scores, qs[:, r, a], km[:, r, a], start=True, stop=False)
                        last = t.matmul(scores, ones_b[0:SPLITS, 0:64],
                                        bias_row[:, r].rearrange("s (h a t) -> s h a t", h=HEADS, a=2)[:, :, a],
                                        start=False, stop=True)
                    last.then_inc(S["score_mm"], 1)
                if live(known, 3, n):
                    pe.wait_ge(S["ctx_copied"], p - 2)
                    if past(known, 4):
                        pe.wait_ge(S["ctxT_done"], p - 3)
                    t.transpose(bank[6][:, 0:P], ctx_sb[:, :], ident[:, :]).then_inc(S["context_turned"], 1)
                if live(known, 1, n):
                    pe.wait_ge(S["xs_copied"], p)
                    if past(known, 2):
                        pe.wait_ge(S["v_done"], p - 1)
                    for a in range(2):
                        last = t.matmul(bank[2][:, a * D:(a + 1) * D], xs[:, 1 - r, a],
                                        wp[:, C_V:C_V + D], start=True, stop=True)
                    last.then_inc(S["v_mm"], 1)
                    pe.wait_ge(S["probs_done"], p)
                    if past(known, 2):
                        pe.wait_ge(S["pT_done"], p - 1)
                    if past(known, 3):
                        pe.wait_ge(S["ctx_copied"], p - 2)
                    for h in range(0, HEADS, 2):
                        last = t.transpose(bank[3][:, h * 64:h * 64 + P],
                                           e_sb[:, 1 - r, h:h + 2].rearrange("p h s -> p (h s)"), ident[:, :])
                    last.then_inc(S["probs_turned"], 1)
                if live(known, 2, n):
                    if known is not None and known > n:
                        pe.wait_ge(S["pT_done"], p - 1)
                        pe.wait_ge(S["ctx_copied"], p - 2)
                    for a in range(2):
                        for h in range(HEADS):
                            o = 64 * (h % 2)
                            last = t.matmul(bank[4 + h % 2][64 * a:64 * a + TOK, (h // 2) * DH:(h // 2 + 1) * DH],
                                            pT[o:o + TOK, r, h // 2, a],
                                            v_sb[o:o + TOK, r, a, h * DH:(h + 1) * DH], start=True, stop=True)
                    last.then_inc(S["context_mm"], 1)
                if live(known, 3, n):
                    pe.wait_ge(S["ctxT_done"], p - 2)
                    if past(known, 4):
                        pe.wait_ge(S["h_added"], p - 3)
                    t.matmul(bank[7][:, 0:PT], wp[:, C_D:C_D + D], ctxT[:, :], start=True, stop=True
                             ).then_inc(S["project_mm"], 1)
            steps(pe, PAIRS, 3, attend)

            def rows_of_h(i, r, known, n):
                pe.wait_ge(S["hs_copied"], i + 1)
                if past(known, 2):
                    pe.wait_ge(S["h_rowed"], i - 1)
                    pe.wait_ge(S["stat_done"], i - 1)
                t.transpose(bank[r][:, 0:P], hs[:, r], ident[:, :]).then_inc(S["h_turned"], 1)
            steps(pe, TILES, 0, rows_of_h)

            def route_rows(i, r, known, n):
                if live(known, 0, n):
                    pe.wait_ge(S["xn_rowed"], i + 1)
                    if past(known, 2):
                        pe.wait_ge(S["xnT_done"], i - 1)
                    t.transpose(bank[2 + r][:, 0:P], xn_row[:, r], ident[:, :]).then_inc(S["xn_turned"], 1)
                if live(known, 1, n):
                    pe.wait_ge(S["xnT_done"], i)
                    if past(known, 3):
                        pe.wait_ge(S["logit_done"], i - 2)
                    t.matmul(bank[5 - r][:, 0:NG + EXPERTS], xnT2[:, 1 - r], wp[:, C_R:C_R + NG + EXPERTS],
                             start=True, stop=True).then_inc(S["logit_mm"], 1)
            steps(pe, TILES, 1, route_rows)

            pe.wait_ge(S["mask_ready"], 1)
            per = 512 // EXPERTS
            regions = TILES + 1
            rank = [bank[k] for k in range(-(-regions // per))]
            for k in range(len(rank)):
                n = min(per, regions - k * per)
                t.matmul(rank[k][:, 0:n * EXPERTS], earlier[:, :], seen[:, k * per:k * per + n], start=True, stop=False,
                         skip_group_check=True)
            for j in range(TILES):
                for k in range(len(rank)):
                    a, b = max(j + 1, k * per), min(regions, (k + 1) * per)
                    if a < b:
                        last = t.matmul(rank[k][:, (a - k * per) * EXPERTS:(b - k * per) * EXPERTS], ones_b[:, :],
                                        seen[:, j].unsqueeze(1).to_broadcast([P, b - a, EXPERTS]),
                                        start=False, stop=(j == TILES - 1), skip_group_check=True)
            last.then_inc(S["rank_mm"], 1)
            pe.wait_ge(S["ecol_ready"], 1)
            for c in range(2):
                last = t.matmul(bank[3][0:1, c * P:(c + 1) * P], e_col[:, c:c + 1], ident[:, :], start=True, stop=True)
            last.then_inc(S["erow_mm"], 1)

            def table(i, first, final, known):
                for k in range(PICKS):
                    pe.wait_ge(S["onehot_done"], i * PICKS + k + 1)
                    t.matmul(bank[4][:, 0:EXPERT_TILES], onehot_slot[:, k], onehot_tile[:, k],
                             start=(first and k == 0), stop=(final and k == PICKS - 1), skip_group_check=True
                             ).then_inc(S["table_mm"], 1)
            table(0, True, False, 0)
            with pe.Fori(1, TILES - 1, 1) as i:
                table(i, False, False, None)
            table(TILES - 1, False, True, TILES - 1)

            pe.wait_ge(S["w1_loaded"], 16)
            pe.wait_ge(S["w2_loaded"], 16)
            pe.wait_ge(S["tiles_known"], 1)
            pe.wait_ge(S["table_done"], 1)

            def expert(j, r, known, n, slot):
                if live(known, 0, n):
                    pe.wait_ge(gathered[slot], (j - slot) * 16 // RING + 16 if known is not None else ring_value(j, slot))
                    if past(known, 2):
                        pe.wait_ge(S["xT_done"], j - 1)
                    t.transpose(bank[r][:, 0:P], xg[:, slot], ident[:, :]).then_inc(S["x_turned"], 1)
                if live(known, 1, n):
                    e = pe.value_load(tile_expert[0:1, ds(j - 1, 1)], min_val=0, max_val=EXPERTS - 1)
                    pe.wait_ge(S["xT_done"], j)
                    if past(known, 3):
                        pe.wait_ge(S["hidden_done"], j - 2)
                    t.matmul(bank[3 - r][:, 0:HID], xgT[:, 1 - r], w1[:, ds(e * HID, HID)], start=True, stop=True
                             ).then_inc(S["hidden_mm"], 1)
                if live(known, 2, n):
                    pe.wait_ge(S["hidden_done"], j - 1)
                    if past(known, 4):
                        pe.wait_ge(S["relu_done"], j - 3)
                    for half in range(2):
                        last = t.transpose(bank[4 + r][:, half * P:half * P + P], hid[:, r, half * P:half * P + P],
                                           ident[:, :])
                    last.then_inc(S["hidden_turned"], 1)
                if live(known, 3, n):
                    e = pe.value_load(tile_expert[0:1, ds(j - 3, 1)], min_val=0, max_val=EXPERTS - 1)
                    pe.wait_ge(S["relu_done"], j - 2)
                    if past(known, 5):
                        pe.wait_ge(S["y_done"], j - 4)
                    for half in range(2):
                        last = t.matmul(bank[7 - r][:, 0:D], hidT[:, 1 - r, half],
                                        w2[:, ds(e * HID + half * D, D)], start=(half == 0), stop=(half == 1))
                    last.then_inc(S["y_mm"], 1)

            def ring_value(j, slot):
                return round_of[0] * 16 + 16

            round_of = [None]
            for j in range(RING):
                expert(j, j % 2, j, EXPERT_TILES, j % RING)
            with pe.Fori(1, EXPERT_TILES // RING, 1) as it:
                round_of[0] = it
                for slot in range(RING):
                    expert(it * RING + slot, slot % 2, None, EXPERT_TILES, slot)
            for j in range(EXPERT_TILES, EXPERT_TILES + 3):
                expert(j, j % 2, j, EXPERT_TILES, j % RING)

            pe.wait_ge(S["b2_loaded"], 16)

            def biases(i, r, known, n):
                pe.wait_ge(S["c_copied"], i + 1)
                if past(known, 2):
                    pe.wait_ge(S["cT_done"], i - 1)
                t.transpose(bank[r][:, 0:P], c_now[:, r].rearrange("p a e -> p (a e)"), ident[:, :]).then_inc(S["c_turned"], 1)
                pe.wait_ge(S["cT_done"], i + 1)
                if past(known, 2):
                    pe.wait_ge(S["base_done"], i - 1)
                t.matmul(bank[2 + r][:, 0:D], cT[:, r], b2[:, :], start=True, stop=True).then_inc(S["b2_mm"], 1)
            steps(pe, TILES, 0, biases)

        @block.vector
        def _(dve):
            v = nc.vector
            dve.wait_ge(S["small_loaded"], 16)
            dve.wait_ge(S["consts_made"], 1)
            v.tensor_copy(hT[:, 0:T].rearrange("p (b t) -> p b t", t=TOK)[:, :, 0],
                          wp[:, C_CLS:C_CLS + 1].to_broadcast([P, IMAGES])).then_inc(S["cls_placed"], 1)
            v.memset(hT[:, T:TP], 0.0)
            v.memset(qT[:, T:TP], 0.0).then_inc(S["pads_done"], 1)

            def embed(i, r, known, n):
                if live(known, 1, n):
                    dve.wait_ge(S["spread_done"], i)
                    if past(known, 2):
                        dve.wait_ge(S["xn_done"], i - 1)
                    v.reciprocal(inv, spread).then_inc(S["inv_done"], 1)
                    dve.wait_ge(S["inv_done"], i)
                    dve.wait_ge(S["center_mm"], i)
                    v.tensor_tensor(xnT[:, ds((i - 1) * GT, GT)], bank[2 - r][:, 0:GT], inv, ALU.mult
                                    ).then_inc(S["xn_done"], 1)
                if live(known, 2, n):
                    dve.wait_ge(S["qk_mm"], i - 1)
                    v.tensor_copy(kT[:, ds((i - 2) * GT, GT)], bank[5][:, 0:GT]).then_inc(S["k_done"], 1)
                    done = (i - 2) * 5
                    if past(known, 3):
                        dve.wait_ge(S["bias_split"], i - 2)

                    def part(n_):
                        return bias_parts[:, n_, ds((i - 2) * GT, GT)]
                    v.tensor_scalar(cb_f, bank[6][0:HEADS, 0:GT], SCALE, None, ALU.mult).then_inc(S["split_step"], 1)
                    dve.wait_ge(S["split_step"], done + 1)
                    v.tensor_copy(part(0), cb_f).then_inc(S["split_step"], 1)
                    dve.wait_ge(S["split_step"], done + 2)
                    v.tensor_tensor(cb_r, cb_f, part(0), ALU.subtract).then_inc(S["split_step"], 1)
                    dve.wait_ge(S["split_step"], done + 3)
                    v.tensor_copy(part(1), cb_r).then_inc(S["split_step"], 1)
                    dve.wait_ge(S["split_step"], done + 4)
                    v.tensor_tensor(cb_m, cb_r, part(1), ALU.subtract).then_inc(S["split_step"], 1)
                    dve.wait_ge(S["split_step"], done + 5)
                    v.tensor_copy(part(2), cb_m).then_inc(S["bias_split"], 1)
            steps(dve, GROUPS_OF_IMAGES, 2, embed)
            dve.wait_ge(S["q_done"], GROUPS_OF_IMAGES)
            dve.wait_ge(S["pads_done"], 1)

            def copies(p, r, again):
                if again:
                    dve.wait_ge(S["score_mm"], p - 1)
                for a in range(2):
                    last = v.tensor_copy(qs[:, r, a], qT[:, ds(p * PT + a * TOK, 64)])
                last.then_inc(S["qs_copied"], 1)

            dve.wait_ge(S["squared"], GROUPS_OF_IMAGES)
            dve.wait_ge(S["var_mm"], GROUPS_OF_IMAGES)
            dve.wait_ge(S["bias_split"], GROUPS_OF_IMAGES)
            v.memset(xs.rearrange("p r a t -> p (r a t)"), 0.0)
            v.memset(e_sb.rearrange("p r h s -> p (r h s)"), 0.0).then_inc(S["pads_done"], 1)
            dve.wait_ge(S["pads_done"], 2)
            copies(0, 0, False)

            def attend(p, r, known, n):
                if live(known, 0, n):
                    if known is None or known + 1 < n:
                        copies(p + 1, 1 - r, known is None or known >= 1)
                    dve.wait_ge(S["score_mm"], p + 1)
                    sc = bank[r][:, 0:HS].rearrange("p (h s) -> p h s", h=HEADS)
                    e = e_sb[:, r, :, 0:TOK]
                    v.tensor_reduce(top[:, r], sc, AX.X, ALU.max).then_inc(S["maxed"], 1)
                    dve.wait_ge(S["maxed"], p + 1)
                    if past(known, 2):
                        dve.wait_ge(S["probs_turned"], p - 1)
                    v.tensor_tensor(e, sc, top[:, r].unsqueeze(2).to_broadcast([P, HEADS, TOK]), ALU.subtract
                                    ).then_inc(S["lessened"], 1)
                    if past(known, 2):
                        dve.wait_ge(S["v_mm"], p - 1)
                    for a in range(2):
                        last = v.tensor_copy(xs[:, r, a].rearrange("p (o t) -> p o t", o=2)[:, :, 0:TOK],
                                             xnT[:, ds(p * PT + a * TOK, TOK)].unsqueeze(1).to_broadcast([P, 2, TOK]))
                    last.then_inc(S["xs_copied"], 1)
                    dve.wait_ge(S["exped"], p + 1)
                    v.tensor_reduce(total[:, r], e_sb[:, r, :, 0:TOK], AX.X, ALU.add
                                    ).then_inc(S["summed"], 1)
                    dve.wait_ge(S["summed"], p + 1)
                    v.reciprocal(inv_total[:, r], total[:, r]).then_inc(S["inverted"], 1)
                if live(known, 3, n):
                    dve.wait_ge(S["project_mm"], p - 2)
                    hp = hT[:, ds((p - 3) * PT, PT)]
                    v.scalar_tensor_tensor(out=hp, in0=bank[7][:, 0:PT], scalar=wp[:, C_BD:C_BD + 1], in1=hp,
                                           op0=ALU.add, op1=ALU.add).then_inc(S["h_added"], 1)
                if live(known, 2, n):
                    dve.wait_ge(S["context_mm"], p - 1)
                    if past(known, 3):
                        dve.wait_ge(S["context_turned"], p - 2)
                    for o in range(2):
                        last = v.tensor_copy(
                            ctx_sb[:, :].rearrange("p (h o d) -> p h o d", o=2, d=DH)[:, :, o],
                            bank[4 + o][:, 0:D // 2].rearrange("p (h d) -> p h d", d=DH))
                    last.then_inc(S["ctx_copied"], 1)
            steps(dve, PAIRS, 3, attend, ahead=1)

            dve.wait_ge(S["h_added"], PAIRS)

            def rows_of_h(i, r, known, n):
                if live(known, 0, n):
                    if past(known, 2):
                        dve.wait_ge(S["h_turned"], i - 1)
                    v.tensor_copy(hs[:, r], hT[:, ds(i * P, P)]).then_inc(S["hs_copied"], 1)
                if live(known, 1, n):
                    dve.wait_ge(S["h_rowed"], i)
                    v.bn_stats(stats[:, ds(i - 1, 1)].rearrange("p i s -> p (i s)"), bank[1 - r][:, 0:P]
                               ).then_inc(S["stat_done"], 1)
            steps(dve, TILES, 1, rows_of_h)
            dve.wait_ge(S["stat_done"], TILES)
            v.tensor_tensor(diff2, stats[:, :, 1], stats[:, :, 4], ALU.subtract)
            v.tensor_tensor(mean2, stats[:, :, 1], stats[:, :, 4], ALU.add)
            v.tensor_tensor(var2, stats[:, :, 2], stats[:, :, 5], ALU.add).then_inc(S["var_step"], 1)
            dve.wait_ge(S["var_step"], 1)
            v.scalar_tensor_tensor(out=diff2, in0=diff2, scalar=D / 4.0, in1=diff2, op0=ALU.mult, op1=ALU.mult)
            v.tensor_scalar(mean2, mean2, 0.5, None, ALU.mult).then_inc(S["var_step"], 1)
            dve.wait_ge(S["var_step"], 2)
            v.tensor_tensor(var2, var2, diff2, ALU.add).then_inc(S["var_step"], 1)
            dve.wait_ge(S["var_step"], 3)
            v.tensor_scalar(var2, var2, 1.0 / D, None, ALU.mult).then_inc(S["var_ready"], 1)
            dve.wait_ge(S["spread2_done"], 1)
            v.reciprocal(rstd2, sd2).then_inc(S["inv2_done"], 1)
            dve.wait_ge(S["inv2_done"], 1)

            def rows_of_xn(i, r, known, n):
                if live(known, 0, n):
                    if past(known, 2):
                        dve.wait_ge(S["xn_turned"], i - 1)
                        dve.wait_ge(xn_stored[r], (i - r) * 8)
                    v.tensor_scalar(xn_row[:, r], h_tok[:, ds(i, 1)].rearrange("p i d -> p (i d)"),
                                    mean2[:, ds(i, 1)], rstd2[:, ds(i, 1)], ALU.subtract, ALU.mult
                                    ).then_inc(S["xn_rowed"], 1)
                if live(known, 2, n):
                    dve.wait_ge(S["logit_mm"], i - 1)
                    v.tensor_copy(logits[:, ds(i - 2, 1)].rearrange("p i e -> p (i e)"), bank[4 + r][:, 0:NG + EXPERTS]
                                  ).then_inc(S["logit_done"], 1)
            steps(dve, TILES, 2, rows_of_xn)

            n_r = [0]

            def link(ins):
                n_r[0] += 1
                ins.then_inc(S["route"], 1)
                dve.wait_ge(S["route"], n_r[0])

            dve.wait_ge(S["logit_done"], TILES)
            for r in range(2):
                dve.wait_ge(xn_stored[r], 16 * ((TILES + 1 - r) // 2))

            def top2(x, n, best_a, best_b, hot_a, hot_b):
                def wide(a):
                    return a.unsqueeze(2).to_broadcast([P, n, NE])
                idx = tmp_i.rearrange("p i a e -> p (i a) e")[:, 0:n]
                rest = tmp_x.rearrange("p i a e -> p (i a) e")[:, 0:n]
                iota = iota8[:, :].unsqueeze(1).to_broadcast([P, n, NE])
                for m, hot in ((best_a, hot_a), (best_b, hot_b)):
                    link(v.tensor_reduce(m, x, AX.X, ALU.max))
                    link(v.tensor_tensor(idx, x, wide(m), ALU.is_equal))
                    link(v.scalar_tensor_tensor(out=idx, in0=idx, scalar=-float(NE), in1=iota, op0=ALU.mult, op1=ALU.add))
                    link(v.tensor_reduce(lowest[:, 0:n], idx, AX.X, ALU.min))
                    link(v.tensor_tensor(hot, idx, wide(lowest[:, 0:n]), ALU.is_equal))
                    if m is best_a:
                        link(v.scalar_tensor_tensor(out=rest, in0=hot, scalar=LOW, in1=x, op0=ALU.mult, op1=ALU.add))
                        x = rest

            def select(big, a, small_out):
                link(v.tensor_tensor(prod, big, oh1[a].unsqueeze(3).to_broadcast([P, TILES, NG, NE]), ALU.mult))
                link(v.tensor_reduce(small_out[:, :, a], prod.rearrange("p i g e -> p i e g"), AX.X, ALU.add))

            l1 = logits[:, :, 0:NG]
            l2 = logits[:, :, NG:NG + EXPERTS].rearrange("p i (g e) -> p i g e", g=NG)
            top2(l1, TILES, best[:, 0, 0, 0:TILES], best[:, 0, 1, 0:TILES], oh1[0], oh1[1])
            for a in range(2):
                select(l2, a, sel)
            flat = [x.rearrange("p i a e -> p (i a) e") for x in (sel, oh2[0], oh2[1])]
            top2(flat[0], 2 * TILES, best[:, 1, 0], best[:, 1, 1], flat[1], flat[2])
            link(v.memset(gap[:, 0, TILES:2 * TILES], 0.0))
            link(v.tensor_tensor(gap[:, 0, 0:TILES], best[:, 0, 1, 0:TILES], best[:, 0, 0, 0:TILES], ALU.subtract))
            v.tensor_tensor(gap[:, 1], best[:, 1, 1], best[:, 1, 0], ALU.subtract).then_inc(S["gap_ready"], 1)
            link(v.tensor_tensor(tmp_x, oh2[0], oh2[1], ALU.add))
            link(v.memset(seen[:, TILES], 0.0))
            call = seen[:, 0:TILES].rearrange("p i (g e) -> p i g e", g=NG)

            def spread_out(out_, a):
                return v.tensor_tensor(out_, oh1[a].unsqueeze(3).to_broadcast([P, TILES, NG, NE]),
                                       tmp_x[:, :, a].unsqueeze(2).to_broadcast([P, TILES, NG, NE]), ALU.mult)
            link(spread_out(call, 0))
            link(spread_out(prod, 1))
            link(v.tensor_tensor(call, call, prod, ALU.add))
            v.memset(seen[LAST:P, TILES - 1], 0.0).then_inc(S["mask_ready"], 1)
            dve.wait_ge(S["exp_ready"], 1)
            link(v.tensor_scalar(den, egap, 1.0, None, ALU.add))
            link(v.reciprocal(share[:, :, 0], den))
            link(v.tensor_tensor(share[:, :, 1], egap, share[:, :, 0], ALU.mult))
            wk = weight.rearrange("p i (a b) -> p i a b", a=2)
            for a in range(2):
                for b in range(2):
                    sh2 = share[:, 1, b, :].rearrange("p (i a) -> p i a", a=2)[:, :, a]
                    last = v.tensor_tensor(wk[:, :, a, b], share[:, 0, a, 0:TILES], sh2, ALU.mult)
            link(last)
            v.memset(cmp, 0.0).then_inc(S["share_ready"], 1)

            dve.wait_ge(S["rank_mm"], 1)
            per = 512 // EXPERTS
            totals = bank[TILES // per][:, (TILES % per) * EXPERTS:(TILES % per + 1) * EXPERTS]
            link(v.tensor_scalar(count_i, totals, float(P - 1), None, ALU.add))
            link(v.tensor_single_scalar(count_s, count_i, 7, ALU.arith_shift_right))
            link(v.tensor_copy(tiles_f, count_s))
            link(v.tensor_tensor_scan(tiles_end, ones_f[:, :], tiles_f, 0.0, ALU.mult, ALU.add))
            for c in range(2):
                link(v.tensor_scalar(cmp, tiles_end, tile_no[:, c:c + 1], None, ALU.is_le))
                ins = v.tensor_reduce(e_col[:, c:c + 1], cmp, AX.X, ALU.add)
                if c == 0:
                    link(ins)
                else:
                    ins.then_inc(S["ecol_ready"], 1)
            link(v.tensor_tensor(base_e, tiles_end, tiles_f, ALU.subtract))
            link(v.tensor_scalar(base_e, base_e, float(P), None, ALU.mult))
            for k in range(-(-TILES // per)):
                n = min(per, TILES - k * per)
                last = v.tensor_tensor(prod[:, k * per:k * per + n].rearrange("p i g e -> p i (g e)"),
                                       bank[k][:, 0:n * EXPERTS].rearrange("p (i e) -> p i e", e=EXPERTS),
                                       base_e.unsqueeze(1).to_broadcast([P, n, EXPERTS]), ALU.add)
            link(last)
            dve.wait_ge(S["step_c"], 6)
            big = logits[:, :, NG:NG + EXPERTS].rearrange("p i (g e) -> p i g e", g=NG)
            pos4 = pos_f.rearrange("p i (a b) -> p i a b", a=2)
            for a in range(2):
                link(v.tensor_tensor(big, prod, oh1[a].unsqueeze(3).to_broadcast([P, TILES, NG, NE]), ALU.mult))
                ins = v.tensor_reduce(tmp_i[:, :, a], big.rearrange("p i g e -> p i e g"), AX.X, ALU.add)
                if a == 1:
                    ins.then_inc(S["rank_read"], 1)
                    dve.wait_ge(S["rank_read"], 1)
                else:
                    link(ins)
            for b in range(2):
                link(v.tensor_tensor(tmp_x, tmp_i, oh2[b], ALU.mult))
                link(v.tensor_reduce(pos4[:, :, :, b], tmp_x, AX.X, ALU.add))
            link(v.tensor_scalar(pos_f, pos_f, float(SLOTS - 1), None, ALU.min))
            link(v.tensor_copy(pos_i, pos_f))
            link(v.tensor_single_scalar(hi_i, pos_i, 7, ALU.arith_shift_right))
            link(v.tensor_copy(hi_f, hi_i))
            link(v.scalar_tensor_tensor(out=lo_f, in0=hi_f, scalar=-float(P), in1=pos_f, op0=ALU.mult, op1=ALU.add))
            dve.wait_ge(S["erow_mm"], 1)
            v.tensor_scalar(tile_expert, bank[3][0:1, 0:2 * P], float(EXPERTS - 1), None, ALU.min
                            ).then_inc(S["tiles_known"], 1)

            def one_hots(i, again):
                for k in range(PICKS):
                    if again:
                        dve.wait_ge(S["table_mm"], (i - 1) * PICKS + k + 1)
                    v.tensor_scalar(onehot_slot[:, k], iota_slot[:, :],
                                    lo_f[:, ds(i, 1), k], None, ALU.is_equal)
                    v.tensor_scalar(onehot_tile[:, k], iota_tile[:, :], hi_f[:, ds(i, 1), k],
                                    tok_val[:, ds(i, 1)], ALU.is_equal, ALU.mult).then_inc(S["onehot_done"], 1)
            one_hots(0, False)
            with dve.Fori(1, TILES, 1) as i:
                one_hots(i, True)
            dve.wait_ge(S["table_mm"], TILES * PICKS)
            v.tensor_scalar(slot_token, bank[4][:, 0:EXPERT_TILES], float(MID), None, ALU.add
                            ).then_inc(S["table_done"], 1)
            dve.wait_ge(S["table_done"], 1)
            dve.wait_ge(S["c_ready"], 1)

            def idx_copy(j, slot):
                v.tensor_copy(idx_now[:, slot:slot + 1], slot_token[:, ds(j, 1)]).then_inc(S["idx_copied"], 1)

            for j in range(RING):
                idx_copy(j, j)

            def expert(j, r, known, n, slot, it):
                if live(known, 1, n):
                    dve.wait_ge(S["hidden_mm"], j)
                    if past(known, 3):
                        dve.wait_ge(S["hidden_turned"], j - 2)
                    v.tensor_copy(hid[:, 1 - r], bank[3 - r][:, 0:HID]).then_inc(S["hidden_done"], 1)
                    if known is None or known - 1 + RING < n:
                        back = (slot - 1) % RING
                        idx_copy(j - 1 + RING, back)
                if live(known, 3, n):
                    dve.wait_ge(S["y_mm"], j - 2)
                    back = (slot - 3) % RING
                    if past(known, RING + 3):
                        dve.wait_ge(y_stored[back], 16 * (it if slot >= 3 else it - 1))
                    v.tensor_copy(y_sb[:, back], bank[7 - r][:, 0:D]).then_inc(S["y_done"], 1)

            for j in range(2 * RING):
                expert(j, j % 2, j, EXPERT_TILES, j % RING, j // RING)
            with dve.Fori(2, EXPERT_TILES // RING - 1, 1) as it:
                for slot in range(RING):
                    expert(it * RING + slot, slot % 2, None, EXPERT_TILES, slot, it)
            for j in range(EXPERT_TILES - RING, EXPERT_TILES + 3):
                expert(j, j % 2, j, EXPERT_TILES, j % RING, j // RING)

            for r in range(RING):
                dve.wait_ge(y_stored[r], 16 * (EXPERT_TILES // RING))

            def pos_copy(i, r):
                v.tensor_copy(pos_now[:, r], pos_i[:, ds(i, 1)].rearrange("p i k -> p (i k)")).then_inc(S["pos_copied"], 1)

            pos_copy(0, 0)
            pos_copy(1, 1)

            def combine(i, r, known, n):
                dve.wait_ge(S["b2_mm"], i + 1)
                if past(known, 2):
                    dve.wait_ge(out_stored[r], (i - r) * 8)
                v.tensor_tensor(acc[:, r], bank[2 + r][:, 0:D], h_tok[:, ds(i, 1)].rearrange("p i d -> p (i d)"), ALU.add
                                ).then_inc(S["base_done"], 1)
                dve.wait_ge(S["base_done"], i + 1)
                dve.wait_ge(y_fetched[r], (i - r) * 8 * PICKS + 16 * PICKS)
                for k in range(PICKS):
                    ins = v.scalar_tensor_tensor(out=acc[:, r], in0=y_got[:, r, k],
                                                 scalar=weight[:, ds(i, 1), k], in1=acc[:, r], op0=ALU.mult, op1=ALU.add)
                    if k < PICKS - 1:
                        ins.then_inc(S["acc_step"], 1)
                        dve.wait_ge(S["acc_step"], i * (PICKS - 1) + k + 1)
                    else:
                        ins.then_inc(S["acc_done"], 1)
                if known is None or known + 2 < n:
                    pos_copy(i + 2, r)
            for i in range(2):
                combine(i, i % 2, i, TILES)
            with dve.Fori(1, (TILES - 3) // 2, 1) as turn:
                i = turn * 2
                combine(i, 0, None, TILES)
                combine(i + 1, 1, None, TILES)
            for i in range(TILES - 3, TILES):
                combine(i, i % 2, i, TILES)


def kernel(x, cls_tok, L0_tok_w, L0_tok_b, L0_attn_Wq, L0_attn_Wk, L0_attn_Wv, L0_attn_Wb, L0_attn_mixing, L0_attn_Wd,
           L0_attn_bd, L0_ffn_g1, L0_ffn_g2, L0_ffn_W1, L0_ffn_b1, L0_ffn_W2, L0_ffn_b2):
    import numpy as np
    import concourse.bacc as bacc
    from concourse.bass_utils import run_bass_kernel_spmd

    a = np.asarray
    px = a(x).reshape(IMAGES, 3, 6, 16, 6, 16).transpose(1, 3, 5, 0, 2, 4).reshape(K_CHUNKS, P, GROUPS_OF_IMAGES, GP)
    px = px.transpose(2, 1, 0, 3)
    small = np.concatenate([
        a(L0_tok_w).T.reshape(K_CHUNKS, P, D).transpose(1, 0, 2).reshape(P, K_CHUNKS * D),
        a(L0_attn_Wq).T, a(L0_attn_Wk).T, a(L0_attn_Wv).T, a(L0_attn_Wd).T,
        a(L0_ffn_g1), a(L0_ffn_g2).transpose(1, 0, 2).reshape(D, EXPERTS),
        a(L0_attn_Wb).T, a(L0_attn_mixing).T,
        a(L0_ffn_b1).reshape(EXPERTS * 2, P).T,
        a(L0_tok_b).reshape(D, 1), a(cls_tok).reshape(D, 1), a(L0_attn_bd).reshape(D, 1)], axis=1)
    w1 = a(L0_ffn_W1).reshape(EXPERTS, D, HID).transpose(1, 0, 2).reshape(D, EXPERTS * HID)
    w2 = a(L0_ffn_W2).reshape(EXPERTS, 2, P, D).transpose(2, 0, 1, 3).reshape(P, EXPERTS * HID)
    b2 = a(L0_ffn_b2).reshape(EXPERTS, D)
    arrays = {"patches_in": px, "small_in": small, "w1_in": w1, "w2_in": w2, "b2_in": b2}
    arrays = {k: np.ascontiguousarray(v) for k, v in arrays.items()}

    nc = bacc.Bacc("TRN2", target_bir_lowering=False, num_devices=1)
    aps = [nc.dram_tensor(k, v.shape, mybir.dt.from_np(v.dtype), kind="ExternalInput").ap() for k, v in arrays.items()]
    out = nc.dram_tensor("out", [IMAGES, TOK, D], F32, kind="ExternalOutput").ap()
    build(nc, *aps, out)
    r = run_bass_kernel_spmd(nc, [arrays], core_ids=[0])
    return r.results[0]["out"]
```

```python
from contextlib import ExitStack

import concourse.bass as bass
from concourse import mybir

P = 128
IMAGES = 64
PATCHES = 36
TOK = PATCHES + 1
D = 128
K_CHUNKS = 3 * 16 * 16 // P
HEADS = 8
DH = D // HEADS
T = IMAGES * TOK
TILES = -(-T // P)
TP = TILES * P
LAST = T - (TILES - 1) * P
GROUP = 8
GROUPS_OF_IMAGES = IMAGES // GROUP
GP = GROUP * PATCHES
GT = GROUP * TOK
PAIRS = IMAGES // 2
PT = 2 * TOK
HS = HEADS * TOK
NG = 8
NE = 8
EXPERTS = NG * NE
HID = 2 * D
PICKS = 4
EXPERT_TILES = T * PICKS // P + EXPERTS
SLOTS = EXPERT_TILES * P
RING = 6
SPLITS = 3
EPS = 1e-5
SCALE = (D / HEADS) ** -0.5
MID = T // 2
LOW = -3.0e38

C_TOKW = 0
C_Q = C_TOKW + K_CHUNKS * P
C_K = C_Q + D
C_V = C_K + D
C_D = C_V + D
C_R = C_D + D
C_B = C_R + NG + EXPERTS
C_MIX = C_B + HEADS
C_B1 = C_MIX + HEADS
C_TOKB = C_B1 + 2 * EXPERTS
C_CLS = C_TOKB + 1
C_BD = C_CLS + 1
C_ALL = C_BD + 1

ALU = mybir.AluOpType
ACT = mybir.ActivationFunctionType
AX = mybir.AxisListType
F32 = mybir.dt.float32
BF16 = mybir.dt.bfloat16
FP16 = mybir.dt.float16
I32 = mybir.dt.int32
ds = bass.ds


def build(nc, patches, small, w1_dram, w2_dram, b2_dram, out):
    assert T * PICKS % P == 0 and EXPERT_TILES % RING == 0 and PAIRS % 2 == 0 and GROUPS_OF_IMAGES % 2 == 0
    with ExitStack() as ctx:
        def sb(name, shape, dt=F32):
            return ctx.enter_context(nc.sbuf_tensor(name, shape, dt))

        def sem(name):
            return ctx.enter_context(nc.semaphore(name))

        bank = [ctx.enter_context(nc.psum_tensor(f"bank{i}", [P, 512], F32)) for i in range(8)]

        bias_dram = nc.dram_tensor("bias_dram", [SPLITS, HEADS, T], BF16, kind="Internal").ap()
        xn_dram = nc.dram_tensor("xn_dram", [TP, D], F32, kind="Internal").ap()
        y_dram = nc.dram_tensor("y_dram", [SLOTS, D], F32, kind="Internal").ap()

        w1 = sb("w1", [P, EXPERTS * HID])
        w2 = sb("w2", [P, EXPERTS * HID])
        b2 = sb("b2", [EXPERTS, D])
        wp = sb("wp", [P, C_ALL])
        ident = sb("ident", [P, P])
        center = sb("center", [P, P])
        average = sb("average", [P, P])
        earlier = sb("earlier", [P, P], BF16)
        ones_b = sb("ones_b", [P, P], BF16)
        ones_f = sb("ones_f", [P, EXPERTS])
        eps = sb("eps", [P, 1])
        iota8 = sb("iota8", [P, NE])
        iota_slot = sb("iota_slot", [P, P], FP16)
        iota_tile = sb("iota_tile", [P, EXPERT_TILES], FP16)
        tile_no = sb("tile_no", [P, 2])
        tok_val = sb("tok_val", [P, TILES])
        hT = sb("hT", [P, TP])

        arena_words = 14400
        arena = sb("arena", [P, arena_words])
        used = [0]

        def at(shape, dt=F32):
            n = 1
            for s in shape[1:]:
                n *= s
            words = n if dt in (F32, I32) else -(-n // 2)
            a = arena[0:shape[0], used[0]:used[0] + words]
            used[0] += words
            assert used[0] <= arena_words, used[0]
            if dt != F32:
                a = a.bitcast(dt)
            if len(shape) > 2:
                names = "abcd"[:len(shape) - 1]
                a = a.rearrange("p (" + " ".join(names) + ") -> p " + " ".join(names),
                                **{k: s for k, s in zip(names, shape[1:])})
            return a

        xnT = at([P, T])
        qT = at([P, TP])
        kT = at([P, T])
        used_ab = used[0]
        x_sb = w2[:, 0:K_CHUNKS * GP * GROUPS_OF_IMAGES].rearrange("p (g c n) -> p g c n", c=K_CHUNKS, n=GP)
        bias_parts = w1[0:HEADS, 0:SPLITS * T // 2].bitcast(BF16).rearrange("p (s t) -> p s t", s=SPLITS)
        squares = at([P, GT])
        spread = at([P, GT])
        inv = at([P, GT])
        cb_f = at([HEADS, GT])
        cb_r = at([HEADS, GT])
        cb_m = at([HEADS, GT])
        used[0] = used_ab
        xs = at([P, 2, 2, P])
        qs = at([P, 2, 2, 64])
        km = at([P, 2, 2, HS])
        bias_row = at([SPLITS, 2, HEADS * PT], BF16)
        v_sb = at([P, 2, 2, D])
        e_sb = at([P, 2, HEADS, 64])
        top = at([P, 2, HEADS])
        total = at([P, 2, HEADS])
        inv_total = at([P, 2, HEADS])
        used_b = used[0]

        pT = sb("pT", [P, 2, HEADS // 2, 2, TOK])
        ctx_sb = sb("ctx_sb", [P, D])
        ctxT = sb("ctxT", [P, PT])

        used[0] = 0
        h_tok = at([P, TILES, D])
        logits = at([P, TILES, NG + EXPERTS])
        base_e = at([P, EXPERTS])
        c_all = at([P, TILES, EXPERTS])
        weight = at([P, TILES, PICKS])
        pos_i = at([P, TILES, PICKS], I32)
        slot_token = at([P, EXPERT_TILES], I32)
        tile_expert = at([1, 2 * P], I32)
        used_c = used[0]
        stats = at([P, TILES, 6])
        mean2 = at([P, TILES])
        var2 = at([P, TILES])
        diff2 = at([P, TILES])
        sd2 = at([P, TILES])
        rstd2 = at([P, TILES])
        hs = at([P, 2, P])
        xn_row = at([P, 2, D])
        xnT2 = at([P, 2, P])
        used[0] = used_c
        prod = at([P, TILES, NG, NE])
        seen = at([P, TILES + 1, EXPERTS], BF16)
        oh1 = [at([P, TILES, NG]) for _ in range(2)]
        sel = at([P, TILES, 2, NE])
        oh2 = [at([P, TILES, 2, NE]) for _ in range(2)]
        tmp_x = at([P, TILES, 2, NE])
        tmp_i = at([P, TILES, 2, NE])
        best = at([P, 2, 2, TILES * 2])
        lowest = at([P, TILES * 2])
        gap = at([P, 2, TILES * 2])
        egap = at([P, 2, TILES * 2])
        den = at([P, 2, TILES * 2])
        share = at([P, 2, 2, TILES * 2])
        count_i = at([P, EXPERTS], I32)
        count_s = at([P, EXPERTS], I32)
        tiles_f = at([P, EXPERTS])
        tiles_end = at([P, EXPERTS])
        cmp = at([P, EXPERTS])
        e_col = at([P, 2])
        pos_f = at([P, TILES, PICKS])
        hi_i = at([P, TILES, PICKS], I32)
        hi_f = at([P, TILES, PICKS])
        lo_f = at([P, TILES, PICKS])
        onehot_slot = at([P, 2, PICKS, P], FP16)
        onehot_tile = at([P, 2, PICKS, EXPERT_TILES], FP16)
        used[0] = used_c
        idx_now = at([P, RING], I32)
        xg = at([P, RING, D])
        xgT = at([P, 2, P])
        hid = at([P, 2, HID])
        hidT = at([P, 2, 2, P])
        y_sb = at([P, RING, D])
        used[0] = used_c
        pos_now = at([P, 2, PICKS], I32)
        y_got = at([P, 2, PICKS, D])
        c_now = at([P, 2, 2, EXPERTS])
        cT = at([EXPERTS, 2, P])
        acc = at([P, 2, D])

        S = {n: sem(n) for n in """
            small_loaded b2_loaded w1_loaded w2_loaded bias_stored xn_stored_a xn_stored_b out_stored_a out_stored_b
            x_loaded_a x_loaded_b bias_loaded_a bias_loaded_b
            identity_made consts_made pool_step cls_placed
            embed_mm h_placed center_mm squared var_mm spread_done inv_done xn_done qk_mm q_done k_done
            bias_scaled high_done high_left middle_done middle_left bias_split
            xs_copied qs_copied km_done score_mm v_mm v_done maxed lessened exped summed inverted probs_done
            probs_turned pT_done context_mm ctx_copied context_turned ctxT_done project_mm h_added pads_done
            hs_copied h_turned h_rowed stat_done var_step var_ready spread2_done inv2_done xn_rowed xn_turned xnT_done logit_mm logit_done
            route gap_ready exp_ready mask_ready rank_mm c_ready share_ready step_c ecol_ready erow_mm tiles_known
            onehot_done table_mm table_done rank_read
            idx_copied x_turned xT_done hidden_mm hidden_done hidden_turned relu_done y_mm y_done
            pos_copied c_copied c_turned cT_done b2_mm base_done acc_step acc_done""".split()}
        gathered = [sem(f"gathered{r}") for r in range(RING)]
        y_stored = [sem(f"y_stored{r}") for r in range(RING)]
        y_fetched = [sem(f"y_fetched{r}") for r in range(2)]
        x_loaded = [S["x_loaded_a"], S["x_loaded_b"]]
        bias_loaded = [S["bias_loaded_a"], S["bias_loaded_b"]]
        xn_stored = [S["xn_stored_a"], S["xn_stored_b"]]
        out_stored = [S["out_stored_a"], S["out_stored_b"]]

        def steps(eng, n, lag, step, ahead=0):
            first = (lag + 3) // 2 * 2
            last = n - ahead - (n - ahead - first) % 2
            for i in range(first):
                step(i, i % 2, i, n)
            if last > first:
                with_loop(eng, first, last, 2, lambda i: (step(i, 0, None, n), step(i + 1, 1, None, n)))
            for i in range(last, n + lag):
                step(i, i % 2, i, n)

        def with_loop(eng, a, b, stride, body):
            with eng.Fori(a // stride, b // stride, 1) as n:
                body(n * stride)

        def live(known, lag, n):
            return known is None or 0 <= known - lag < n

        def past(known, m):
            return known is None or known >= m

        def ahead_by_lag(eng, lags):
            for name, lag in lags.items():
                eng.sem_inc(S[name], lag)

        def expert_steps(eng, step, lags):
            deep = max(lags)
            low = min(lags)

            def turn_of(turn, known):
                j0 = turn * RING
                if known is None or known >= RING:
                    count = RING + deep - low
                    _, e = nc.values_load_multi_w_load_instructions(
                        tile_expert[0:1, ds(j0 - deep, count)], engines=(eng.engine,), min_val=0, max_val=EXPERTS - 1)
                    first = -deep
                elif known == 0:
                    count = RING - low
                    _, e = nc.values_load_multi_w_load_instructions(
                        tile_expert[0:1, 0:count], engines=(eng.engine,), min_val=0, max_val=EXPERTS - 1)
                    first = 0
                for slot in range(RING):
                    k = None if known is None else known + slot
                    if k is not None and k >= EXPERT_TILES + deep:
                        break
                    mine = [e[slot - lag - first] if 0 <= slot - lag - first < len(e) else None for lag in lags]
                    step(j0 + slot, slot % 2, k, EXPERT_TILES, slot, turn, *mine)
            turn_of(0, 0)
            with eng.Fori(1, EXPERT_TILES // RING, 1) as it:
                turn_of(it, None)
            turn_of(EXPERT_TILES // RING, EXPERT_TILES)

        block = ctx.enter_context(nc.Block())

        @block.sync
        def _(sp):
            sp.dma_start(wp[:, :], small).then_inc(S["small_loaded"], 16)
            for g in range(2):
                sp.dma_start(x_sb[:, g], patches[g]).then_inc(x_loaded[g], 16)
            with sp.Fori(1, GROUPS_OF_IMAGES // 2, 1) as turn:
                g = turn * 2
                for r in range(2):
                    sp.wait_ge(x_loaded[r], g * 8)
                    sp.dma_start(x_sb[:, ds(g + r, 1)], patches[ds(g + r, 1)].rearrange("g p c n -> p g c n")
                                 ).then_inc(x_loaded[r], 16)
            sp.dma_start(b2[:, :], b2_dram).then_inc(S["b2_loaded"], 16)
            sp.wait_ge(S["bias_split"], GROUPS_OF_IMAGES + 2)
            for s in range(SPLITS):
                sp.dma_start(bias_dram[s], bias_parts[:, s]).then_inc(S["bias_stored"], 16)
            sp.wait_ge(S["bias_stored"], 16 * SPLITS)
            pieces = PAIRS // 2
            piece = EXPERTS * HID // pieces

            def load_weights(k):
                sp.dma_start(w1[:, ds(k * piece, piece)], w1_dram[:, ds(k * piece, piece)]).then_inc(S["w1_loaded"], 16)
                sp.dma_start(w2[:, ds(k * piece, piece)], w2_dram[:, ds(k * piece, piece)]).then_inc(S["w2_loaded"], 16)

            for r in range(2):
                sp.dma_start(bias_row[:, r].rearrange("s (h t) -> s h t", h=HEADS),
                             bias_dram[:, :, r * PT:(r + 1) * PT]).then_inc(bias_loaded[r], 16)
            load_weights(0)
            with sp.Fori(1, PAIRS // 2, 1) as turn:
                p = turn * 2
                for r in range(2):
                    sp.wait_ge(S["score_mm"], p + r - 1)
                    sp.dma_start(bias_row[:, r].rearrange("s (h t) -> s h t", h=HEADS),
                                 bias_dram[:, :, ds((p + r) * PT, PT)]).then_inc(bias_loaded[r], 16)
                load_weights(turn)
            def store_xn(i, r):
                sp.wait_ge(S["xn_rowed"], i + 1)
                sp.dma_start(xn_dram[ds(i * P, P)], xn_row[:, r]).then_inc(xn_stored[r], 16)
            with sp.Fori(0, (TILES - 1) // 2, 1) as turn:
                i = turn * 2
                store_xn(i, 0)
                store_xn(i + 1, 1)
            store_xn(TILES - 1, 0)
            with sp.Fori(0, EXPERT_TILES // RING, 1) as turn:
                j = turn * RING
                for r in range(RING):
                    sp.wait_ge(S["y_done"], j + r + 1 + 3)
                    sp.dma_start(y_dram[ds((j + r) * P, P)], y_sb[:, r]).then_inc(y_stored[r], 16)
            rows = out.rearrange("b s d -> (b s) d")
            with sp.Fori(0, (TILES - 1) // 2, 1) as turn:
                i = turn * 2
                for r in range(2):
                    sp.wait_ge(S["acc_done"], i + r + 1)
                    sp.dma_start(rows[ds((i + r) * P, P)], acc[:, r]).then_inc(out_stored[r], 16)
            sp.wait_ge(S["acc_done"], TILES)
            sp.dma_start(rows[(TILES - 1) * P:T], acc[0:LAST, 0]).then_inc(out_stored[0], 16)
            sp.wait_ge(out_stored[0], 16 * (TILES // 2 + 1))
            sp.wait_ge(out_stored[1], 16 * (TILES // 2))

        @block.gpsimd
        def _(pool):
            g = nc.gpsimd
            g.memset(ident[:, :], 0.0)
            g.memset(earlier[:, :], 1.0)
            g.memset(tok_val[:, :], 0.0)
            g.memset(average[:, :], 1.0 / D).then_inc(S["pool_step"], 1)
            pool.wait_ge(S["pool_step"], 1)
            g.affine_select(out=ident[:, :], in_=ident[:, :], compare_op=ALU.not_equal, fill=1.0, base=0,
                            pattern=[[-1, P]], channel_multiplier=1).then_inc(S["pool_step"], 1)
            g.affine_select(out=earlier[:, :], in_=earlier[:, :], compare_op=ALU.is_gt, fill=0.0, base=0,
                            pattern=[[1, P]], channel_multiplier=-1)
            pool.wait_ge(S["pool_step"], 2)
            g.tensor_scalar(center[:, :], ident[:, :], 1.0 / D, None, ALU.subtract)
            g.memset(ones_b[:, :], 1.0)
            g.memset(ones_f[:, :], 1.0)
            g.memset(ctx_sb[:, :], 0.0)
            g.memset(eps[:, :], EPS)
            g.iota(iota8[:, :], pattern=[[1, NE]], base=0, channel_multiplier=0, allow_small_or_imprecise_dtypes=True)
            g.iota(iota_slot[:, :], pattern=[[1, P]], base=0, channel_multiplier=0, allow_small_or_imprecise_dtypes=True)
            g.iota(iota_tile[:, :], pattern=[[1, EXPERT_TILES]], base=0, channel_multiplier=0,
                   allow_small_or_imprecise_dtypes=True)
            g.iota(tile_no[:, :], pattern=[[P, 2]], base=0, channel_multiplier=1, allow_small_or_imprecise_dtypes=True)
            g.iota(tok_val[:, 0:TILES - 1], pattern=[[P, TILES - 1]], base=-MID, channel_multiplier=1,
                   allow_small_or_imprecise_dtypes=True)
            g.iota(tok_val[0:LAST, TILES - 1:TILES], pattern=[[P, 1]], base=(TILES - 1) * P - MID, channel_multiplier=1,
                   allow_small_or_imprecise_dtypes=True).then_inc(S["consts_made"], 1)

            mix = wp[:, C_MIX:C_MIX + HEADS].unsqueeze(2).to_broadcast([P, HEADS, TOK])

            def mix_keys(p, r):
                for a in range(2):
                    last = g.tensor_tensor(
                        km[:, r, a].rearrange("p (h s) -> p h s", h=HEADS),
                        kT[:, ds(p * PT + a * TOK, TOK)].unsqueeze(1).to_broadcast([P, HEADS, TOK]), mix, ALU.mult)
                last.then_inc(S["km_done"], 1)

            pool.wait_ge(S["bias_split"], GROUPS_OF_IMAGES + 2)
            pool.wait_ge(S["k_done"], GROUPS_OF_IMAGES + 2)
            mix_keys(0, 0)

            def attend(p, r, known, n):
                if known is None or known + 1 < n:
                    if past(known, 1):
                        pool.wait_ge(S["score_mm"], p)
                    mix_keys(p + 1, 1 - r)
                pool.wait_ge(S["inverted"], p + 1)
                e = e_sb[:, r, :, 0:TOK]
                g.tensor_tensor(e, e, inv_total[:, r].unsqueeze(2).to_broadcast([P, HEADS, TOK]), ALU.mult
                                ).then_inc(S["probs_done"], 1)
            steps(pool, PAIRS, 0, attend, ahead=1)

            pool.wait_ge(S["share_ready"], 1)
            n_c = [0]

            def link(ins):
                n_c[0] += 1
                ins.then_inc(S["step_c"], 1)
                pool.wait_ge(S["step_c"], n_c[0])

            def bc(a, shape):
                return a.to_broadcast(shape)

            sh2 = [share[:, 1, b, :].rearrange("p (i a) -> p i a", a=2).unsqueeze(3) for b in range(2)]
            link(g.tensor_tensor(sel, oh2[0], bc(sh2[0], [P, TILES, 2, NE]), ALU.mult))
            link(g.tensor_tensor(tmp_x, oh2[1], bc(sh2[1], [P, TILES, 2, NE]), ALU.mult))
            link(g.tensor_tensor(sel, sel, tmp_x, ALU.add))
            for a in range(2):
                sh1 = share[:, 0, a, 0:TILES].unsqueeze(2)
                link(g.tensor_tensor(sel[:, :, a], sel[:, :, a], bc(sh1, [P, TILES, NE]), ALU.mult))
            call = c_all.rearrange("p i (g e) -> p i g e", g=NG)
            link(g.tensor_tensor(call, bc(oh1[0].unsqueeze(3), [P, TILES, NG, NE]),
                                 bc(sel[:, :, 0].unsqueeze(2), [P, TILES, NG, NE]), ALU.mult))
            pool.wait_ge(S["rank_read"], 1)
            link(g.tensor_tensor(prod, bc(oh1[1].unsqueeze(3), [P, TILES, NG, NE]),
                                 bc(sel[:, :, 1].unsqueeze(2), [P, TILES, NG, NE]), ALU.mult))
            g.tensor_tensor(call, call, prod, ALU.add).then_inc(S["c_ready"], 1)

            for r in range(2):
                pool.wait_ge(xn_stored[r], 16 * ((TILES + 1 - r) // 2))

            def gather(j, r, again):
                copied = j + r + 1 if not again else pool.to_reg(j + r + 1)
                pool.wait_ge(S["table_done"], 1)
                pool.wait_ge(S["idx_copied"], copied)
                g.indirect_dma_start(xg[:, r], None, xn_dram, bass.IndirectOffsetOnAxis(idx_now[:, r:r + 1], 0)
                                     ).then_inc(gathered[r], 16)
            for r in range(RING):
                gather(0, r, False)
            with pool.Fori(1, EXPERT_TILES // RING, 1) as turn:
                j = turn * RING
                for r in range(RING):
                    gather(j, r, True)

            for r in range(RING):
                pool.wait_ge(y_stored[r], 16 * (EXPERT_TILES // RING))

            def fetch(i, r, again):
                copied = i + 1 if not again else pool.to_reg(i + 1)
                pool.wait_ge(S["table_done"], 1)
                pool.wait_ge(S["pos_copied"], copied)
                for k in range(PICKS):
                    g.indirect_dma_start(y_got[:, r, k], None, y_dram,
                                         bass.IndirectOffsetOnAxis(pos_now[:, r, k:k + 1], 0)).then_inc(y_fetched[r], 16)
            fetch(0, 0, False)
            fetch(1, 1, False)
            with pool.Fori(1, (TILES - 1) // 2, 1) as turn:
                i = turn * 2
                fetch(i, 0, True)
                fetch(i + 1, 1, True)
            fetch(TILES - 1, 0, True)

        @block.scalar
        def _(act):
            s = nc.scalar
            act.wait_ge(S["small_loaded"], 16)
            act.wait_ge(S["consts_made"], 1)

            ahead_by_lag(act, {"spread_done": 1, "q_done": 2})

            def embed(i, r, known, n):
                if live(known, 0, n):
                    act.wait_ge(S["embed_mm"], i + 1)
                    s.activation(hT[:, ds(i * GT, GT)].rearrange("p (b t) -> p b t", t=TOK)[:, :, 1:TOK],
                                 bank[0][:, 0:GP].rearrange("p (b t) -> p b t", t=PATCHES), ACT.Identity,
                                 bias=wp[:, C_TOKB:C_TOKB + 1]).then_inc(S["h_placed"], 1)
                if live(known, 2, n):
                    act.wait_ge(S["qk_mm"], i + 1)
                    s.activation(qT[:, ds((i - 2) * GT, GT)], bank[4][:, 0:GT], ACT.Copy, scale=SCALE
                                 ).then_inc(S["q_done"], 1)
                if live(known, 1, n):
                    act.wait_ge(S["var_mm"], i + 1)
                    s.activation(spread, bank[3][:, 0:GT], ACT.Sqrt, bias=eps[:, :]).then_inc(S["spread_done"], 1)
                if live(known, 0, n):
                    act.wait_ge(S["center_mm"], i + 1)
                    s.activation(squares, bank[1 + r][:, 0:GT], ACT.Square).then_inc(S["squared"], 1)
            steps(act, GROUPS_OF_IMAGES, 2, embed)

            ahead_by_lag(act, {"v_done": 1, "pT_done": 1, "ctxT_done": 3})

            def attend(p, r, known, n):
                if live(known, 3, n):
                    act.wait_ge(S["context_turned"], p + 1)
                    s.activation(ctxT[:, :].rearrange("p (a t) -> p a t", a=2),
                                 bank[6][:, 0:P].rearrange("p (a t) -> p a t", a=2)[:, :, 0:TOK], ACT.Copy
                                 ).then_inc(S["ctxT_done"], 1)
                if live(known, 1, n):
                    act.wait_ge(S["v_mm"], p + 1)
                    s.activation(v_sb[:, 1 - r], bank[2][:, 0:2 * D].rearrange("p (a d) -> p a d", a=2), ACT.Copy
                                 ).then_inc(S["v_done"], 1)
                    act.wait_ge(S["probs_turned"], p + 1)
                    s.activation(pT[:, 1 - r],
                                 bank[3][:, :].rearrange("p (h a t) -> p h a t", h=4, a=2)[:, :, :, 0:TOK],
                                 ACT.Copy).then_inc(S["pT_done"], 1)
                if live(known, 0, n):
                    act.wait_ge(S["lessened"], p + 1)
                    s.activation(e_sb[:, r, :, 0:TOK], e_sb[:, r, :, 0:TOK], ACT.Exp).then_inc(S["exped"], 1)
            steps(act, PAIRS, 3, attend)

            act.wait_ge(S["h_added"], PAIRS + 3)

            def rows_of_h(i, r, known, n):
                act.wait_ge(S["h_turned"], i + 1)
                s.activation(h_tok[:, ds(i, 1)].rearrange("p i d -> p (i d)"), bank[r][:, 0:P], ACT.Copy
                             ).then_inc(S["h_rowed"], 1)
            steps(act, TILES, 0, rows_of_h)
            act.wait_ge(S["var_ready"], 1)
            s.activation(sd2, var2, ACT.Sqrt, bias=eps[:, :]).then_inc(S["spread2_done"], 1)

            def rows_of_xn(i, r, known, n):
                act.wait_ge(S["xn_turned"], i + 1)
                if past(known, 2):
                    act.wait_ge(S["logit_mm"], i - 1)
                s.activation(xnT2[:, r], bank[2 + r][:, 0:P], ACT.Copy).then_inc(S["xnT_done"], 1)
            steps(act, TILES, 0, rows_of_xn)

            act.wait_ge(S["gap_ready"], 1)
            s.activation(egap, gap, ACT.Exp).then_inc(S["exp_ready"], 1)

            act.wait_ge(S["tiles_known"], 1)

            ahead_by_lag(act, {"relu_done": 2})

            def expert(j, r, known, n, slot, turn, e):
                if live(known, 0, n):
                    act.wait_ge(S["x_turned"], j + 1)
                    s.activation(xgT[:, r], bank[r][:, 0:P], ACT.Copy).then_inc(S["xT_done"], 1)
                if live(known, 2, n):
                    act.wait_ge(S["hidden_turned"], j + 1)
                    for half in range(2):
                        last = s.activation(hidT[:, r, half], bank[4 + r][:, half * P:half * P + P], ACT.Relu,
                                            bias=wp[:, ds(C_B1 + 2 * e + half, 1)])
                    last.then_inc(S["relu_done"], 1)
            expert_steps(act, expert, [2])

            act.wait_ge(S["c_ready"], 1)
            for r in range(RING):
                act.wait_ge(y_stored[r], 16 * (EXPERT_TILES // RING))

            def biases(i, r, known, n):
                if live(known, 0, n):
                    if past(known, 2):
                        act.wait_ge(S["c_turned"], i - 1)
                    s.activation(c_now[:, r], c_all[:, ds(i, 1)].to_broadcast([P, 2, EXPERTS]), ACT.Copy
                                 ).then_inc(S["c_copied"], 1)
                    act.wait_ge(S["c_turned"], i + 1)
                    if past(known, 2):
                        act.wait_ge(S["b2_mm"], i - 1)
                    s.activation(cT[:, r], bank[r][0:EXPERTS, 0:P], ACT.Copy).then_inc(S["cT_done"], 1)
            steps(act, TILES, 0, biases)

        @block.tensor
        def _(pe):
            t = nc.tensor
            pe.wait_ge(S["small_loaded"], 16)
            pe.wait_ge(S["consts_made"], 1)

            ahead_by_lag(pe, {"var_mm": 1, "qk_mm": 2})
            pe.wait_ge(S["cls_placed"], 1)

            def embed(i, r, known, n):
                if live(known, 0, n):
                    pe.wait_ge(x_loaded[r], (i - r) * 8 + 16)
                    for c in range(K_CHUNKS):
                        last = t.matmul(bank[0][:, 0:GP], wp[:, C_TOKW + c * P:C_TOKW + (c + 1) * P],
                                        x_sb[:, ds(i, 1), c].rearrange("p g n -> p (g n)"),
                                        start=(c == 0), stop=(c == K_CHUNKS - 1))
                    last.then_inc(S["embed_mm"], 1)
                if live(known, 2, n):
                    pe.wait_ge(S["xn_done"], i)
                    xn = xnT[:, ds((i - 2) * GT, GT)]
                    t.matmul(bank[4][:, 0:GT], wp[:, C_Q:C_Q + D], xn, start=True, stop=True)
                    t.matmul(bank[5][:, 0:GT], wp[:, C_K:C_K + D], xn, start=True, stop=True)
                    t.matmul(bank[6][0:HEADS, 0:GT], wp[:, C_B:C_B + HEADS], xn, start=True, stop=True
                             ).then_inc(S["qk_mm"], 1)
                if live(known, 1, n):
                    pe.wait_ge(S["squared"], i)
                    t.matmul(bank[3][:, 0:GT], average[:, :], squares, start=True, stop=True).then_inc(S["var_mm"], 1)
                if live(known, 0, n):
                    pe.wait_ge(S["h_placed"], i + 1)
                    t.matmul(bank[1 + r][:, 0:GT], center[:, :], hT[:, ds(i * GT, GT)], start=True, stop=True
                             ).then_inc(S["center_mm"], 1)
            steps(pe, GROUPS_OF_IMAGES, 2, embed)
            pe.wait_ge(S["q_done"], GROUPS_OF_IMAGES + 2)
            pe.wait_ge(S["k_done"], GROUPS_OF_IMAGES + 2)

            ahead_by_lag(pe, {"v_mm": 1, "probs_turned": 1, "context_mm": 2, "context_turned": 3, "project_mm": 3})

            def attend(p, r, known, n):
                if live(known, 0, n):
                    pe.wait_ge(S["qs_copied"], p + 1)
                    pe.wait_ge(S["km_done"], p + 1)
                    pe.wait_ge(bias_loaded[r], (p - r) * 8 + 16)
                    for a in range(2):
                        scores = bank[r][64 * a:64 * a + 64, 0:HS]
                        t.matmul(scores, qs[:, r, a], km[:, r, a], start=True, stop=False)
                        last = t.matmul(scores, ones_b[0:SPLITS, 0:64],
                                        bias_row[:, r].rearrange("s (h a t) -> s h a t", h=HEADS, a=2)[:, :, a],
                                        start=False, stop=True)
                    last.then_inc(S["score_mm"], 1)
                if live(known, 3, n):
                    pe.wait_ge(S["ctx_copied"], p)
                    t.transpose(bank[6][:, 0:P], ctx_sb[:, :], ident[:, :]).then_inc(S["context_turned"], 1)
                if live(known, 2, n):
                    pe.wait_ge(S["pT_done"], p)
                if live(known, 1, n):
                    pe.wait_ge(S["xs_copied"], p)
                    for a in range(2):
                        last = t.matmul(bank[2][:, a * D:(a + 1) * D], xs[:, 1 - r, a],
                                        wp[:, C_V:C_V + D], start=True, stop=True)
                    last.then_inc(S["v_mm"], 1)
                    pe.wait_ge(S["probs_done"], p)
                    for h in range(0, HEADS, 2):
                        last = t.transpose(bank[3][:, h * 64:h * 64 + P],
                                           e_sb[:, 1 - r, h:h + 2].rearrange("p h s -> p (h s)"), ident[:, :])
                    last.then_inc(S["probs_turned"], 1)
                if live(known, 3, n):
                    pe.wait_ge(S["ctxT_done"], p + 1)
                    t.matmul(bank[7][:, 0:PT], wp[:, C_D:C_D + D], ctxT[:, :], start=True, stop=True
                             ).then_inc(S["project_mm"], 1)
                if live(known, 2, n):
                    for a in range(2):
                        for h in range(HEADS):
                            o = 64 * (h % 2)
                            last = t.matmul(bank[4 + h % 2][64 * a:64 * a + TOK, (h // 2) * DH:(h // 2 + 1) * DH],
                                            pT[o:o + TOK, r, h // 2, a],
                                            v_sb[o:o + TOK, r, a, h * DH:(h + 1) * DH], start=True, stop=True)
                    last.then_inc(S["context_mm"], 1)
            steps(pe, PAIRS, 3, attend)

            def rows_of_h(i, r, known, n):
                pe.wait_ge(S["hs_copied"], i + 1)
                if past(known, 2):
                    pe.wait_ge(S["h_rowed"], i - 1)
                    pe.wait_ge(S["stat_done"], i - 1)
                t.transpose(bank[r][:, 0:P], hs[:, r], ident[:, :]).then_inc(S["h_turned"], 1)
            steps(pe, TILES, 0, rows_of_h)

            def route_rows(i, r, known, n):
                if live(known, 0, n):
                    pe.wait_ge(S["xn_rowed"], i + 1)
                    if past(known, 2):
                        pe.wait_ge(S["xnT_done"], i - 1)
                    t.transpose(bank[2 + r][:, 0:P], xn_row[:, r], ident[:, :]).then_inc(S["xn_turned"], 1)
                if live(known, 1, n):
                    pe.wait_ge(S["xnT_done"], i)
                    if past(known, 3):
                        pe.wait_ge(S["logit_done"], i - 2)
                    t.matmul(bank[5 - r][:, 0:NG + EXPERTS], xnT2[:, 1 - r], wp[:, C_R:C_R + NG + EXPERTS],
                             start=True, stop=True).then_inc(S["logit_mm"], 1)
            steps(pe, TILES, 1, route_rows)

            pe.wait_ge(S["mask_ready"], 1)
            per = 512 // EXPERTS
            regions = TILES + 1
            rank = [bank[k] for k in range(-(-regions // per))]
            for k in range(len(rank)):
                n = min(per, regions - k * per)
                t.matmul(rank[k][:, 0:n * EXPERTS], earlier[:, :], seen[:, k * per:k * per + n], start=True, stop=False,
                         skip_group_check=True)
            for j in range(TILES):
                for k in range(len(rank)):
                    a, b = max(j + 1, k * per), min(regions, (k + 1) * per)
                    if a < b:
                        last = t.matmul(rank[k][:, (a - k * per) * EXPERTS:(b - k * per) * EXPERTS], ones_b[:, :],
                                        seen[:, j].unsqueeze(1).to_broadcast([P, b - a, EXPERTS]),
                                        start=False, stop=(j == TILES - 1), skip_group_check=True)
            last.then_inc(S["rank_mm"], 1)
            pe.wait_ge(S["ecol_ready"], 1)
            for c in range(2):
                last = t.matmul(bank[3][0:1, c * P:(c + 1) * P], e_col[:, c:c + 1], ident[:, :], start=True, stop=True)
            last.then_inc(S["erow_mm"], 1)

            def table(i, r, known, n):
                pe.wait_ge(S["onehot_done"], i + 1)
                for k in range(PICKS):
                    last = t.matmul(bank[4][:, 0:EXPERT_TILES], onehot_slot[:, r, k], onehot_tile[:, r, k],
                                    start=(known == 0 and k == 0), stop=(known == n - 1 and k == PICKS - 1),
                                    skip_group_check=True)
                last.then_inc(S["table_mm"], 1)
            steps(pe, TILES, 0, table)

            pe.wait_ge(S["w1_loaded"], 16 * (PAIRS // 2))
            pe.wait_ge(S["w2_loaded"], 16 * (PAIRS // 2))
            pe.wait_ge(S["tiles_known"], 1)
            pe.wait_ge(S["table_done"], 1)

            ahead_by_lag(pe, {"hidden_mm": 1, "hidden_turned": 2, "y_mm": 3})

            def expert(j, r, known, n, slot, turn, e1, e3):
                if live(known, 0, n):
                    pe.wait_ge(gathered[slot], turn * 16 + 16)
                    t.transpose(bank[r][:, 0:P], xg[:, slot], ident[:, :]).then_inc(S["x_turned"], 1)
                if live(known, 1, n):
                    pe.wait_ge(S["xT_done"], j)
                    t.matmul(bank[3 - r][:, 0:HID], xgT[:, 1 - r], w1[:, ds(e1 * HID, HID)], start=True, stop=True
                             ).then_inc(S["hidden_mm"], 1)
                if live(known, 2, n):
                    pe.wait_ge(S["hidden_done"], j)
                    for half in range(2):
                        last = t.transpose(bank[4 + r][:, half * P:half * P + P], hid[:, r, half * P:half * P + P],
                                           ident[:, :])
                    last.then_inc(S["hidden_turned"], 1)
                if live(known, 3, n):
                    if not live(known, 2, n):
                        pe.wait_ge(S["y_done"], j - 1)
                    pe.wait_ge(S["relu_done"], j)
                    for half in range(2):
                        last = t.matmul(bank[7 - r][:, 0:D], hidT[:, 1 - r, half],
                                        w2[:, ds(e3 * HID + half * D, D)], start=(half == 0), stop=(half == 1))
                    last.then_inc(S["y_mm"], 1)
            expert_steps(pe, expert, [1, 3])

            pe.wait_ge(S["b2_loaded"], 16)

            def biases(i, r, known, n):
                pe.wait_ge(S["c_copied"], i + 1)
                if past(known, 2):
                    pe.wait_ge(S["cT_done"], i - 1)
                t.transpose(bank[r][:, 0:P], c_now[:, r].rearrange("p a e -> p (a e)"), ident[:, :]).then_inc(S["c_turned"], 1)
                pe.wait_ge(S["cT_done"], i + 1)
                if past(known, 2):
                    pe.wait_ge(S["base_done"], i - 1)
                t.matmul(bank[2 + r][:, 0:D], cT[:, r], b2[:, :], start=True, stop=True).then_inc(S["b2_mm"], 1)
            steps(pe, TILES, 0, biases)

        @block.vector
        def _(dve):
            v = nc.vector
            dve.wait_ge(S["small_loaded"], 16)
            dve.wait_ge(S["consts_made"], 1)
            v.tensor_copy(hT[:, 0:T].rearrange("p (b t) -> p b t", t=TOK)[:, :, 0],
                          wp[:, C_CLS:C_CLS + 1].to_broadcast([P, IMAGES])).then_inc(S["cls_placed"], 1)
            v.memset(hT[:, T:TP], 0.0)
            v.memset(qT[:, T:TP], 0.0).then_inc(S["pads_done"], 1)

            ahead_by_lag(dve, {"inv_done": 1, "xn_done": 1, "k_done": 2, "bias_scaled": 2, "high_done": 2,
                               "high_left": 2, "middle_done": 2, "middle_left": 2, "bias_split": 2})

            def embed(i, r, known, n):
                if live(known, 2, n):
                    dve.wait_ge(S["qk_mm"], i + 1)
                    v.tensor_copy(kT[:, ds((i - 2) * GT, GT)], bank[5][:, 0:GT]).then_inc(S["k_done"], 1)

                    def part(n_):
                        return bias_parts[:, n_, ds((i - 2) * GT, GT)]
                    v.tensor_scalar(cb_f, bank[6][0:HEADS, 0:GT], SCALE, None, ALU.mult).then_inc(S["bias_scaled"], 1)
                    dve.wait_ge(S["bias_scaled"], i + 1)
                    v.tensor_copy(part(0), cb_f).then_inc(S["high_done"], 1)
                    dve.wait_ge(S["high_done"], i + 1)
                    v.tensor_tensor(cb_r, cb_f, part(0), ALU.subtract).then_inc(S["high_left"], 1)
                    dve.wait_ge(S["high_left"], i + 1)
                    v.tensor_copy(part(1), cb_r).then_inc(S["middle_done"], 1)
                    dve.wait_ge(S["middle_done"], i + 1)
                    v.tensor_tensor(cb_m, cb_r, part(1), ALU.subtract).then_inc(S["middle_left"], 1)
                    dve.wait_ge(S["middle_left"], i + 1)
                    v.tensor_copy(part(2), cb_m).then_inc(S["bias_split"], 1)
                if live(known, 1, n):
                    dve.wait_ge(S["spread_done"], i + 1)
                    v.reciprocal(inv, spread).then_inc(S["inv_done"], 1)
                    dve.wait_ge(S["inv_done"], i + 1)
                    v.tensor_tensor(xnT[:, ds((i - 1) * GT, GT)], bank[2 - r][:, 0:GT], inv, ALU.mult
                                    ).then_inc(S["xn_done"], 1)
            steps(dve, GROUPS_OF_IMAGES, 2, embed)
            dve.wait_ge(S["q_done"], GROUPS_OF_IMAGES + 2)
            dve.wait_ge(S["pads_done"], 1)

            def copies(p, r):
                for a in range(2):
                    last = v.tensor_copy(qs[:, r, a], qT[:, ds(p * PT + a * TOK, 64)])
                last.then_inc(S["qs_copied"], 1)

            dve.wait_ge(S["squared"], GROUPS_OF_IMAGES)
            dve.wait_ge(S["var_mm"], GROUPS_OF_IMAGES + 1)
            dve.wait_ge(S["bias_split"], GROUPS_OF_IMAGES + 2)
            v.memset(xs.rearrange("p r a t -> p (r a t)"), 0.0)
            v.memset(e_sb.rearrange("p r h s -> p (r h s)"), 0.0).then_inc(S["pads_done"], 1)
            dve.wait_ge(S["pads_done"], 2)
            copies(0, 0)
            ahead_by_lag(dve, {"h_added": 3, "ctx_copied": 2})

            def attend(p, r, known, n):
                if live(known, 0, n):
                    if known is None or known + 1 < n:
                        copies(p + 1, 1 - r)
                    dve.wait_ge(S["score_mm"], p + 1)
                    sc = bank[r][:, 0:HS].rearrange("p (h s) -> p h s", h=HEADS)
                    e = e_sb[:, r, :, 0:TOK]
                    v.tensor_reduce(top[:, r], sc, AX.X, ALU.max).then_inc(S["maxed"], 1)
                    dve.wait_ge(S["maxed"], p + 1)
                    v.tensor_tensor(e, sc, top[:, r].unsqueeze(2).to_broadcast([P, HEADS, TOK]), ALU.subtract
                                    ).then_inc(S["lessened"], 1)
                    for a in range(2):
                        last = v.tensor_copy(xs[:, r, a].rearrange("p (o t) -> p o t", o=2)[:, :, 0:TOK],
                                             xnT[:, ds(p * PT + a * TOK, TOK)].unsqueeze(1).to_broadcast([P, 2, TOK]))
                    last.then_inc(S["xs_copied"], 1)
                    dve.wait_ge(S["exped"], p + 1)
                    v.tensor_reduce(total[:, r], e_sb[:, r, :, 0:TOK], AX.X, ALU.add
                                    ).then_inc(S["summed"], 1)
                    dve.wait_ge(S["summed"], p + 1)
                    v.reciprocal(inv_total[:, r], total[:, r]).then_inc(S["inverted"], 1)
                if live(known, 3, n):
                    dve.wait_ge(S["project_mm"], p + 1)
                    hp = hT[:, ds((p - 3) * PT, PT)]
                    v.scalar_tensor_tensor(out=hp, in0=bank[7][:, 0:PT], scalar=wp[:, C_BD:C_BD + 1], in1=hp,
                                           op0=ALU.add, op1=ALU.add).then_inc(S["h_added"], 1)
                if live(known, 2, n):
                    dve.wait_ge(S["context_mm"], p + 1)
                    for o in range(2):
                        last = v.tensor_copy(
                            ctx_sb[:, :].rearrange("p (h o d) -> p h o d", o=2, d=DH)[:, :, o],
                            bank[4 + o][:, 0:D // 2].rearrange("p (h d) -> p h d", d=DH))
                    last.then_inc(S["ctx_copied"], 1)
            steps(dve, PAIRS, 3, attend, ahead=1)

            dve.wait_ge(S["h_added"], PAIRS + 3)

            def rows_of_h(i, r, known, n):
                if live(known, 0, n):
                    if past(known, 2):
                        dve.wait_ge(S["h_turned"], i - 1)
                    v.tensor_copy(hs[:, r], hT[:, ds(i * P, P)]).then_inc(S["hs_copied"], 1)
                if live(known, 1, n):
                    dve.wait_ge(S["h_rowed"], i)
                    v.bn_stats(stats[:, ds(i - 1, 1)].rearrange("p i s -> p (i s)"), bank[1 - r][:, 0:P]
                               ).then_inc(S["stat_done"], 1)
            steps(dve, TILES, 1, rows_of_h)
            dve.wait_ge(S["stat_done"], TILES)
            v.tensor_tensor(diff2, stats[:, :, 1], stats[:, :, 4], ALU.subtract)
            v.tensor_tensor(mean2, stats[:, :, 1], stats[:, :, 4], ALU.add)
            v.tensor_tensor(var2, stats[:, :, 2], stats[:, :, 5], ALU.add).then_inc(S["var_step"], 1)
            dve.wait_ge(S["var_step"], 1)
            v.scalar_tensor_tensor(out=diff2, in0=diff2, scalar=D / 4.0, in1=diff2, op0=ALU.mult, op1=ALU.mult)
            v.tensor_scalar(mean2, mean2, 0.5, None, ALU.mult).then_inc(S["var_step"], 1)
            dve.wait_ge(S["var_step"], 2)
            v.tensor_tensor(var2, var2, diff2, ALU.add).then_inc(S["var_step"], 1)
            dve.wait_ge(S["var_step"], 3)
            v.tensor_scalar(var2, var2, 1.0 / D, None, ALU.mult).then_inc(S["var_ready"], 1)
            dve.wait_ge(S["spread2_done"], 1)
            v.reciprocal(rstd2, sd2).then_inc(S["inv2_done"], 1)
            dve.wait_ge(S["inv2_done"], 1)

            def rows_of_xn(i, r, known, n):
                if live(known, 0, n):
                    if past(known, 2):
                        dve.wait_ge(S["xn_turned"], i - 1)
                        dve.wait_ge(xn_stored[r], (i - r) * 8)
                    v.tensor_scalar(xn_row[:, r], h_tok[:, ds(i, 1)].rearrange("p i d -> p (i d)"),
                                    mean2[:, ds(i, 1)], rstd2[:, ds(i, 1)], ALU.subtract, ALU.mult
                                    ).then_inc(S["xn_rowed"], 1)
                if live(known, 2, n):
                    dve.wait_ge(S["logit_mm"], i - 1)
                    v.tensor_copy(logits[:, ds(i - 2, 1)].rearrange("p i e -> p (i e)"), bank[4 + r][:, 0:NG + EXPERTS]
                                  ).then_inc(S["logit_done"], 1)
            steps(dve, TILES, 2, rows_of_xn)

            n_r = [0]

            def link(ins):
                n_r[0] += 1
                ins.then_inc(S["route"], 1)
                dve.wait_ge(S["route"], n_r[0])

            dve.wait_ge(S["logit_done"], TILES)
            for r in range(2):
                dve.wait_ge(xn_stored[r], 16 * ((TILES + 1 - r) // 2))

            def top2(x, n, best_a, best_b, hot_a, hot_b):
                def wide(a):
                    return a.unsqueeze(2).to_broadcast([P, n, NE])
                idx = tmp_i.rearrange("p i a e -> p (i a) e")[:, 0:n]
                rest = tmp_x.rearrange("p i a e -> p (i a) e")[:, 0:n]
                iota = iota8[:, :].unsqueeze(1).to_broadcast([P, n, NE])
                for m, hot in ((best_a, hot_a), (best_b, hot_b)):
                    link(v.tensor_reduce(m, x, AX.X, ALU.max))
                    link(v.tensor_tensor(idx, x, wide(m), ALU.is_equal))
                    link(v.scalar_tensor_tensor(out=idx, in0=idx, scalar=-float(NE), in1=iota, op0=ALU.mult, op1=ALU.add))
                    link(v.tensor_reduce(lowest[:, 0:n], idx, AX.X, ALU.min))
                    link(v.tensor_tensor(hot, idx, wide(lowest[:, 0:n]), ALU.is_equal))
                    if m is best_a:
                        link(v.scalar_tensor_tensor(out=rest, in0=hot, scalar=LOW, in1=x, op0=ALU.mult, op1=ALU.add))
                        x = rest

            def select(big, a, small_out):
                link(v.tensor_tensor(prod, big, oh1[a].unsqueeze(3).to_broadcast([P, TILES, NG, NE]), ALU.mult))
                link(v.tensor_reduce(small_out[:, :, a], prod.rearrange("p i g e -> p i e g"), AX.X, ALU.add))

            l1 = logits[:, :, 0:NG]
            l2 = logits[:, :, NG:NG + EXPERTS].rearrange("p i (g e) -> p i g e", g=NG)
            top2(l1, TILES, best[:, 0, 0, 0:TILES], best[:, 0, 1, 0:TILES], oh1[0], oh1[1])
            for a in range(2):
                select(l2, a, sel)
            flat = [x.rearrange("p i a e -> p (i a) e") for x in (sel, oh2[0], oh2[1])]
            top2(flat[0], 2 * TILES, best[:, 1, 0], best[:, 1, 1], flat[1], flat[2])
            link(v.memset(gap[:, 0, TILES:2 * TILES], 0.0))
            link(v.tensor_tensor(gap[:, 0, 0:TILES], best[:, 0, 1, 0:TILES], best[:, 0, 0, 0:TILES], ALU.subtract))
            v.tensor_tensor(gap[:, 1], best[:, 1, 1], best[:, 1, 0], ALU.subtract).then_inc(S["gap_ready"], 1)
            link(v.tensor_tensor(tmp_x, oh2[0], oh2[1], ALU.add))
            link(v.memset(seen[:, TILES], 0.0))
            call = seen[:, 0:TILES].rearrange("p i (g e) -> p i g e", g=NG)

            def spread_out(out_, a):
                return v.tensor_tensor(out_, oh1[a].unsqueeze(3).to_broadcast([P, TILES, NG, NE]),
                                       tmp_x[:, :, a].unsqueeze(2).to_broadcast([P, TILES, NG, NE]), ALU.mult)
            link(spread_out(call, 0))
            link(spread_out(prod, 1))
            link(v.tensor_tensor(call, call, prod, ALU.add))
            v.memset(seen[LAST:P, TILES - 1], 0.0).then_inc(S["mask_ready"], 1)
            dve.wait_ge(S["exp_ready"], 1)
            link(v.tensor_scalar(den, egap, 1.0, None, ALU.add))
            link(v.reciprocal(share[:, :, 0], den))
            link(v.tensor_tensor(share[:, :, 1], egap, share[:, :, 0], ALU.mult))
            wk = weight.rearrange("p i (a b) -> p i a b", a=2)
            for a in range(2):
                for b in range(2):
                    sh2 = share[:, 1, b, :].rearrange("p (i a) -> p i a", a=2)[:, :, a]
                    last = v.tensor_tensor(wk[:, :, a, b], share[:, 0, a, 0:TILES], sh2, ALU.mult)
            link(last)
            v.memset(cmp, 0.0).then_inc(S["share_ready"], 1)

            dve.wait_ge(S["rank_mm"], 1)
            per = 512 // EXPERTS
            totals = bank[TILES // per][:, (TILES % per) * EXPERTS:(TILES % per + 1) * EXPERTS]
            link(v.tensor_scalar(count_i, totals, float(P - 1), None, ALU.add))
            link(v.tensor_single_scalar(count_s, count_i, 7, ALU.arith_shift_right))
            link(v.tensor_copy(tiles_f, count_s))
            link(v.tensor_tensor_scan(tiles_end, ones_f[:, :], tiles_f, 0.0, ALU.mult, ALU.add))
            for c in range(2):
                link(v.tensor_scalar(cmp, tiles_end, tile_no[:, c:c + 1], None, ALU.is_le))
                ins = v.tensor_reduce(e_col[:, c:c + 1], cmp, AX.X, ALU.add)
                if c == 0:
                    link(ins)
                else:
                    ins.then_inc(S["ecol_ready"], 1)
            link(v.tensor_tensor(base_e, tiles_end, tiles_f, ALU.subtract))
            link(v.tensor_scalar(base_e, base_e, float(P), None, ALU.mult))
            for k in range(-(-TILES // per)):
                n = min(per, TILES - k * per)
                last = v.tensor_tensor(prod[:, k * per:k * per + n].rearrange("p i g e -> p i (g e)"),
                                       bank[k][:, 0:n * EXPERTS].rearrange("p (i e) -> p i e", e=EXPERTS),
                                       base_e.unsqueeze(1).to_broadcast([P, n, EXPERTS]), ALU.add)
            link(last)
            dve.wait_ge(S["step_c"], 6)
            big = logits[:, :, NG:NG + EXPERTS].rearrange("p i (g e) -> p i g e", g=NG)
            pos4 = pos_f.rearrange("p i (a b) -> p i a b", a=2)
            for a in range(2):
                link(v.tensor_tensor(big, prod, oh1[a].unsqueeze(3).to_broadcast([P, TILES, NG, NE]), ALU.mult))
                ins = v.tensor_reduce(tmp_i[:, :, a], big.rearrange("p i g e -> p i e g"), AX.X, ALU.add)
                if a == 1:
                    ins.then_inc(S["rank_read"], 1)
                    dve.wait_ge(S["rank_read"], 1)
                else:
                    link(ins)
            for b in range(2):
                link(v.tensor_tensor(tmp_x, tmp_i, oh2[b], ALU.mult))
                link(v.tensor_reduce(pos4[:, :, :, b], tmp_x, AX.X, ALU.add))
            link(v.tensor_scalar(pos_f, pos_f, float(SLOTS - 1), None, ALU.min))
            link(v.tensor_copy(pos_i, pos_f))
            link(v.tensor_single_scalar(hi_i, pos_i, 7, ALU.arith_shift_right))
            link(v.tensor_copy(hi_f, hi_i))
            link(v.scalar_tensor_tensor(out=lo_f, in0=hi_f, scalar=-float(P), in1=pos_f, op0=ALU.mult, op1=ALU.add))
            dve.wait_ge(S["erow_mm"], 1)
            v.tensor_scalar(tile_expert, bank[3][0:1, 0:2 * P], float(EXPERTS - 1), None, ALU.min
                            ).then_inc(S["tiles_known"], 1)

            def one_hots(i, r, known, n):
                if past(known, 2):
                    dve.wait_ge(S["table_mm"], i - 1)
                for k in range(PICKS):
                    v.tensor_scalar(onehot_slot[:, r, k], iota_slot[:, :], lo_f[:, ds(i, 1), k], None, ALU.is_equal)
                    last = v.tensor_scalar(onehot_tile[:, r, k], iota_tile[:, :], hi_f[:, ds(i, 1), k],
                                           tok_val[:, ds(i, 1)], ALU.is_equal, ALU.mult)
                last.then_inc(S["onehot_done"], 1)
            steps(dve, TILES, 0, one_hots)
            dve.wait_ge(S["table_mm"], TILES)
            v.tensor_scalar(slot_token, bank[4][:, 0:EXPERT_TILES], float(MID), None, ALU.add
                            ).then_inc(S["table_done"], 1)
            dve.wait_ge(S["table_done"], 1)
            dve.wait_ge(S["c_ready"], 1)

            def idx_copy(j, slot):
                v.tensor_copy(idx_now[:, slot:slot + 1], slot_token[:, ds(j, 1)]).then_inc(S["idx_copied"], 1)

            for j in range(RING):
                idx_copy(j, j)

            ahead_by_lag(dve, {"hidden_done": 1, "y_done": 3})

            def expert(j, r, known, n, slot, it):
                if live(known, 1, n):
                    dve.wait_ge(S["hidden_mm"], j + 1)
                    v.tensor_copy(hid[:, 1 - r], bank[3 - r][:, 0:HID]).then_inc(S["hidden_done"], 1)
                    if known is None or known - 1 + RING < n:
                        back = (slot - 1) % RING
                        idx_copy(j - 1 + RING, back)
                if live(known, 3, n):
                    back = (slot - 3) % RING
                    if past(known, RING + 3):
                        dve.wait_ge(y_stored[back], 16 * (it if slot >= 3 else it - 1))
                    dve.wait_ge(S["y_mm"], j + 1)
                    v.tensor_copy(y_sb[:, back], bank[7 - r][:, 0:D]).then_inc(S["y_done"], 1)

            for j in range(2 * RING):
                expert(j, j % 2, j, EXPERT_TILES, j % RING, j // RING)
            with dve.Fori(2, EXPERT_TILES // RING - 1, 1) as it:
                for slot in range(RING):
                    expert(it * RING + slot, slot % 2, None, EXPERT_TILES, slot, it)
            for j in range(EXPERT_TILES - RING, EXPERT_TILES + 3):
                expert(j, j % 2, j, EXPERT_TILES, j % RING, j // RING)

            for r in range(RING):
                dve.wait_ge(y_stored[r], 16 * (EXPERT_TILES // RING))

            def pos_copy(i, r):
                v.tensor_copy(pos_now[:, r], pos_i[:, ds(i, 1)].rearrange("p i k -> p (i k)")).then_inc(S["pos_copied"], 1)

            pos_copy(0, 0)
            pos_copy(1, 1)

            def combine(i, r, known, n):
                dve.wait_ge(S["b2_mm"], i + 1)
                if past(known, 2):
                    dve.wait_ge(out_stored[r], (i - r) * 8)
                v.tensor_tensor(acc[:, r], bank[2 + r][:, 0:D], h_tok[:, ds(i, 1)].rearrange("p i d -> p (i d)"), ALU.add
                                ).then_inc(S["base_done"], 1)
                dve.wait_ge(S["base_done"], i + 1)
                dve.wait_ge(y_fetched[r], (i - r) * 8 * PICKS + 16 * PICKS)
                for k in range(PICKS):
                    ins = v.scalar_tensor_tensor(out=acc[:, r], in0=y_got[:, r, k],
                                                 scalar=weight[:, ds(i, 1), k], in1=acc[:, r], op0=ALU.mult, op1=ALU.add)
                    if k < PICKS - 1:
                        ins.then_inc(S["acc_step"], 1)
                        dve.wait_ge(S["acc_step"], i * (PICKS - 1) + k + 1)
                    else:
                        ins.then_inc(S["acc_done"], 1)
                if known is None or known + 2 < n:
                    pos_copy(i + 2, r)
            for i in range(2):
                combine(i, i % 2, i, TILES)
            with dve.Fori(1, (TILES - 3) // 2, 1) as turn:
                i = turn * 2
                combine(i, 0, None, TILES)
                combine(i + 1, 1, None, TILES)
            for i in range(TILES - 3, TILES):
                combine(i, i % 2, i, TILES)


def kernel(x, cls_tok, L0_tok_w, L0_tok_b, L0_attn_Wq, L0_attn_Wk, L0_attn_Wv, L0_attn_Wb, L0_attn_mixing, L0_attn_Wd,
           L0_attn_bd, L0_ffn_g1, L0_ffn_g2, L0_ffn_W1, L0_ffn_b1, L0_ffn_W2, L0_ffn_b2):
    import numpy as np
    import concourse.bacc as bacc
    from concourse.bass_utils import run_bass_kernel_spmd

    a = np.asarray
    px = a(x).reshape(IMAGES, 3, 6, 16, 6, 16).transpose(1, 3, 5, 0, 2, 4).reshape(K_CHUNKS, P, GROUPS_OF_IMAGES, GP)
    px = px.transpose(2, 1, 0, 3)
    small = np.concatenate([
        a(L0_tok_w).T.reshape(K_CHUNKS, P, D).transpose(1, 0, 2).reshape(P, K_CHUNKS * D),
        a(L0_attn_Wq).T, a(L0_attn_Wk).T, a(L0_attn_Wv).T, a(L0_attn_Wd).T,
        a(L0_ffn_g1), a(L0_ffn_g2).transpose(1, 0, 2).reshape(D, EXPERTS),
        a(L0_attn_Wb).T, a(L0_attn_mixing).T,
        a(L0_ffn_b1).reshape(EXPERTS * 2, P).T,
        a(L0_tok_b).reshape(D, 1), a(cls_tok).reshape(D, 1), a(L0_attn_bd).reshape(D, 1)], axis=1)
    w1 = a(L0_ffn_W1).reshape(EXPERTS, D, HID).transpose(1, 0, 2).reshape(D, EXPERTS * HID)
    w2 = a(L0_ffn_W2).reshape(EXPERTS, 2, P, D).transpose(2, 0, 1, 3).reshape(P, EXPERTS * HID)
    b2 = a(L0_ffn_b2).reshape(EXPERTS, D)
    arrays = {"patches_in": px, "small_in": small, "w1_in": w1, "w2_in": w2, "b2_in": b2}
    arrays = {k: np.ascontiguousarray(v) for k, v in arrays.items()}

    nc = bacc.Bacc("TRN2", target_bir_lowering=False, num_devices=1)
    aps = [nc.dram_tensor(k, v.shape, mybir.dt.from_np(v.dtype), kind="ExternalInput").ap() for k, v in arrays.items()]
    out = nc.dram_tensor("out", [IMAGES, TOK, D], F32, kind="ExternalOutput").ap()
    build(nc, *aps, out)
    r = run_bass_kernel_spmd(nc, [arrays], core_ids=[0])
    return r.results[0]["out"]
```

```python
from contextlib import ExitStack

import concourse.bass as bass
from concourse import mybir

P = 128
IMAGES = 64
PATCHES = 36
TOK = PATCHES + 1
D = 128
K_CHUNKS = 3 * 16 * 16 // P
HEADS = 8
DH = D // HEADS
T = IMAGES * TOK
TILES = -(-T // P)
TP = TILES * P
LAST = T - (TILES - 1) * P
GROUP = 8
GROUPS_OF_IMAGES = IMAGES // GROUP
GP = GROUP * PATCHES
GT = GROUP * TOK
PAIRS = IMAGES // 2
PT = 2 * TOK
HS = HEADS * TOK
NG = 8
NE = 8
EXPERTS = NG * NE
HID = 2 * D
W1_COLS = HID + 2
PICKS = 4
EXPERT_TILES = T * PICKS // P + EXPERTS
SLOTS = EXPERT_TILES * P
RING = 6
SPLITS = 3
XN_STORES = 4
GATHERS = 3
AHEAD_PAIRS = 6
EPS = 1e-5
SCALE = (D / HEADS) ** -0.5
MID = T // 2
LOW = -3.0e38

C_TOKW = 0
C_TOKB = C_TOKW + K_CHUNKS * P
C_CLS = C_TOKB + 1
C_Q = C_CLS + 1
C_K = C_Q + D
C_V = C_K + D
C_D = C_V + D
C_R = C_D + D
C_B = C_R + NG + EXPERTS
C_MIX = C_B + HEADS
C_BD = C_MIX + HEADS
C_ALL = C_BD + 1

ALU = mybir.AluOpType
ACT = mybir.ActivationFunctionType
AX = mybir.AxisListType
F32 = mybir.dt.float32
BF16 = mybir.dt.bfloat16
FP16 = mybir.dt.float16
I32 = mybir.dt.int32
ds = bass.ds


def build(nc, patches, small, w1_dram, w2_dram, b2_dram, out):
    assert T * PICKS % P == 0 and EXPERT_TILES % RING == 0 and PAIRS % 2 == 0 and GROUPS_OF_IMAGES % 2 == 0
    with ExitStack() as ctx:
        def sb(name, shape, dt=F32):
            return ctx.enter_context(nc.sbuf_tensor(name, shape, dt))

        def sem(name):
            return ctx.enter_context(nc.semaphore(name))

        bank = [ctx.enter_context(nc.psum_tensor(f"bank{i}", [P, 512], F32)) for i in range(8)]

        bias_dram = nc.dram_tensor("bias_dram", [SPLITS, HEADS, T], BF16, kind="Internal").ap()
        xn_dram = nc.dram_tensor("xn_dram", [TP, D], F32, kind="Internal").ap()
        y_dram = nc.dram_tensor("y_dram", [SLOTS, D], F32, kind="Internal").ap()

        w1 = sb("w1", [P, EXPERTS * W1_COLS])
        w2 = sb("w2", [P, EXPERTS * HID])
        b2 = sb("b2", [EXPERTS, D])
        wp = sb("wp", [P, C_ALL])
        ident = sb("ident", [P, P])
        center = sb("center", [P, P])
        average = sb("average", [P, P])
        not_earlier = sb("not_earlier", [P, P], BF16)
        ones_b = sb("ones_b", [P, P], BF16)
        ones_f = sb("ones_f", [P, EXPERTS])
        eps = sb("eps", [P, 1])
        zero = sb("zero", [HEADS, 1])
        iota8 = sb("iota8", [P, NE])
        tile_no = sb("tile_no", [P, 2])
        tok_val = sb("tok_val", [P, TILES])
        hT = sb("hT", [P, TP])

        arena_words = 14400
        arena = sb("arena", [P, arena_words])
        used = [0]

        def at(shape, dt=F32):
            n = 1
            for s in shape[1:]:
                n *= s
            words = n if dt in (F32, I32) else -(-n // 2)
            a = arena[0:shape[0], used[0]:used[0] + words]
            used[0] += words
            assert used[0] <= arena_words, used[0]
            if dt != F32:
                a = a.bitcast(dt)
            if len(shape) > 2:
                names = "abcd"[:len(shape) - 1]
                a = a.rearrange("p (" + " ".join(names) + ") -> p " + " ".join(names),
                                **{k: s for k, s in zip(names, shape[1:])})
            return a

        xnT = at([P, T])
        qT = at([P, T])
        kT = at([P, T])
        x_sb = w2[:, 0:K_CHUNKS * GP * GROUPS_OF_IMAGES].rearrange("p (g c n) -> p g c n", c=K_CHUNKS, n=GP)
        squares = at([P, GT])
        spread = at([P, 2, GT])
        inv = at([P, GT])
        cb_f = at([HEADS, 2, GT])
        cb_r = at([HEADS, GT])
        cb_m = at([HEADS, GT])
        bias_parts = w1[0:HEADS, 0:SPLITS * GT].bitcast(BF16).rearrange("p (r s t) -> p r s t", r=2, s=SPLITS)
        xs = at([P, 2, 2, P])
        qs = at([P, 2, 2, 64])
        km = at([P, 2, 2, HS])
        bias_row = at([SPLITS, 2, HEADS * PT], BF16)
        v_sb = at([P, 2, 2, D])
        e_sb = at([P, 2, HEADS, 64])
        top = at([P, 2, HEADS])
        total = at([P, 2, HEADS])
        inv_total = at([P, 2, HEADS])

        pT = sb("pT", [P, 2, HEADS // 2, 2, TOK])
        ctx_sb = sb("ctx_sb", [P, D])
        ctxT = sb("ctxT", [P, PT])

        used[0] = 0
        h_tok = at([P, TILES, D])
        logits = at([P, TILES, NG + EXPERTS])
        c_all = at([P, TILES, EXPERTS])
        weight = at([P, TILES, PICKS])
        pos_i = at([P, TILES, PICKS], I32)
        slot_token = at([P, EXPERT_TILES], I32)
        tile_expert = at([1, 2 * P], I32)
        used_c = used[0]
        stats = at([P, 2, 6])
        moments = at([P, 2, 2])
        sd2 = at([P, 2])
        rstd2 = at([P, 2])
        hs = at([P, 2, P])
        xn_now = at([P, 2, D])
        xnT2 = at([P, 2, P])
        used[0] = used_c
        prod = at([P, TILES, NG, NE])
        prod_b = at([P, TILES, NG, NE])
        seen = at([P, EXPERTS, TILES], BF16)
        seen_b = at([P, EXPERTS, TILES], BF16)
        seen_sum = at([P, EXPERTS, TILES], BF16)
        not_first = at([P, EXPERTS, TILES], BF16)
        oh1 = [at([P, TILES, NG]) for _ in range(2)]
        sel = at([P, TILES, 2, NE])
        oh2 = [at([P, TILES, 2, NE]) for _ in range(2)]
        tmp_x = at([P, TILES, 2, NE])
        tmp_i = at([P, TILES, 2, NE])
        best = at([P, 2, 2, TILES * 2])
        lowest = at([P, TILES * 2])
        gap = at([P, 2, TILES * 2])
        egap = at([P, 2, TILES * 2])
        den = at([P, 2, TILES * 2])
        share = at([P, 2, 2, TILES * 2])
        count_i = at([P, EXPERTS], I32)
        count_s = at([P, EXPERTS], I32)
        tiles_f = at([P, EXPERTS])
        tiles_end = at([P, EXPERTS])
        tiles_start = at([P, EXPERTS], BF16)
        cmp = at([P, EXPERTS])
        e_col = at([P, 2])
        pos_f = at([P, TILES, PICKS])
        hi_i = at([P, TILES, PICKS], I32)
        hi_h = at([P, TILES, PICKS], FP16)
        lo_h = at([P, TILES, PICKS], FP16)
        iota_slot = at([P, P, PICKS], FP16)
        iota_tile = at([P, EXPERT_TILES, PICKS], FP16)
        used[0] = used_c
        onehot_slot = at([P, 2, P, PICKS], FP16)
        onehot_tile = at([P, 2, EXPERT_TILES, PICKS], FP16)
        assert used[0] <= used_c + TILES * EXPERTS
        used[0] = used_c + TILES * EXPERTS
        onehot_tok = at([P, 2, EXPERT_TILES, PICKS], FP16)
        assert used[0] <= used_c + 2 * TILES * EXPERTS
        xn_row = hT[:, :].rearrange("p (i d) -> p i d", d=D)
        used[0] = used_c
        idx_now = at([P, RING], I32)
        xg = at([P, RING, D])
        xgT = at([P, 2, P])
        w1_now = at([P, 2, W1_COLS])
        hidT = at([P, 2, 2, P])
        y_sb = at([P, RING, D])
        used[0] = used_c
        pos_now = at([P, 2, PICKS], I32)
        y_got = at([P, 2, PICKS, D])
        c_now = at([P, 2, 2, EXPERTS])
        cT = at([EXPERTS, 2, P])
        acc = at([P, 2, D])

        S = {n: sem(n) for n in """
            embed_loaded small_loaded b2_loaded w1_loaded w2_loaded bias_stored_a bias_stored_b xn_stored out_stored_a out_stored_b
            x_loaded_a x_loaded_b bias_loaded_a bias_loaded_b
            consts_made pool_step cls_placed
            embed_mm h_placed center_mm squared var_mm spread_done inv_done xn_done qk_mm q_done k_done
            bias_scaled high_done high_left middle_done middle_left bias_split
            xs_copied qs_copied km_done score_mm v_mm v_done maxed lessened exped summed inverted
            exps_turned pT_done context_mm ctx_copied context_turned ctxT_done project_mm h_added pads_done
            hs_copied h_turned h_rowed stat_done moments_done sd_done rstd_done xn_rowed xn_kept xn_turned xnT_done logit_mm logit_done
            route tables_made groups_ready product_b_done picked_ready
            gap_ready exp_ready mask_ready totals_mm starts_ready rank_mm c_ready share_ready step_c ecol_ready erow_mm
            tiles_known tiles_onehot slots_onehot weighted_done table_mm table_done
            idx_copied x_turned x_ready hidden_mm relu_done y_mm y_done
            pos_copied c_copied c_turned cT_done b2_mm base_done acc_step acc_done""".split()}
        gathered = [sem(f"gathered{r}") for r in range(RING)]
        y_stored = [sem(f"y_stored{r}") for r in range(RING)]
        y_fetched = [sem(f"y_fetched{r}") for r in range(2)]
        x_loaded = [S["x_loaded_a"], S["x_loaded_b"]]
        bias_stored = [S["bias_stored_a"], S["bias_stored_b"]]
        bias_loaded = [S["bias_loaded_a"], S["bias_loaded_b"]]
        out_stored = [S["out_stored_a"], S["out_stored_b"]]

        def steps(eng, n, lag, step, ahead=0, done=0, turn=2):
            first = -(-(lag + 2) // turn) * turn
            last = n - ahead - (n - ahead - first) % turn
            for i in range(done, first):
                step(i, i % 2, i, n)
            if last > first:
                with_loop(eng, first, last, turn, lambda i: [step(i + k, k % 2, None, n) for k in range(turn)])
            for i in range(last, n + lag):
                step(i, i % 2, i, n)

        def with_loop(eng, a, b, stride, body):
            with eng.Fori(a // stride, b // stride, 1) as n:
                body(n * stride)

        def live(known, lag, n):
            return known is None or 0 <= known - lag < n

        def past(known, m):
            return known is None or known >= m

        def ahead_by_lag(eng, lags):
            for name, lag in lags.items():
                eng.sem_inc(S[name], lag)

        def expert_steps(eng, deep, apart, step):
            for j in range(apart * RING):
                step(j, j, j % RING, j // RING)
            with eng.Fori(apart, EXPERT_TILES // RING, 1) as turn:
                for slot in range(RING):
                    step(turn * RING + slot, None, slot, turn)
            for j in range(EXPERT_TILES, EXPERT_TILES + deep):
                step(j, j, j % RING, j // RING)

        def expert_of(eng, j):
            _, e = nc.values_load_multi_w_load_instructions(
                tile_expert[0:1, ds(j, 1)], engines=(eng.engine,), min_val=0, max_val=EXPERTS - 1,
                skip_runtime_bounds_check_because="VectorE counts at most EXPERTS ends and keeps to EXPERTS - 1")
            return e[0]

        block = ctx.enter_context(nc.Block())

        @block.sync
        def _(sp):
            sp.dma_start(wp[:, 0:C_Q], small[:, 0:C_Q]).then_inc(S["embed_loaded"], 16)
            sp.dma_start(x_sb[:, 0], patches[0]).then_inc(x_loaded[0], 16)
            sp.dma_start(wp[:, C_Q:C_ALL], small[:, C_Q:C_ALL]).then_inc(S["small_loaded"], 16)
            sp.dma_start(x_sb[:, 1], patches[1]).then_inc(x_loaded[1], 16)
            with sp.Fori(1, GROUPS_OF_IMAGES // 2, 1) as turn:
                g = turn * 2
                for r in range(2):
                    sp.wait_ge(x_loaded[r], g * 8)
                    sp.dma_start(x_sb[:, ds(g + r, 1)], patches[ds(g + r, 1)].rearrange("g p c n -> p g c n")
                                 ).then_inc(x_loaded[r], 16)
            sp.dma_start(b2[:, :], b2_dram).then_inc(S["b2_loaded"], 16)
            def store_bias(g, r):
                sp.wait_ge(S["bias_split"], g + 1)
                sp.dma_start(bias_dram[:, :, ds(g * GT, GT)].rearrange("s h t -> h s t"), bias_parts[:, r]
                             ).then_inc(bias_stored[r], 16)
            def load_bias(p, r):
                sp.dma_start(bias_row[:, r].rearrange("s (h t) -> s h t", h=HEADS),
                             bias_dram[:, :, ds(p * PT, PT)]).then_inc(bias_loaded[r], 16)

            store_bias(0, 0)
            sp.wait_ge(bias_stored[0], 16)
            for r in range(2):
                load_bias(r, r)
            store_bias(1, 1)
            with sp.Fori(1, GROUPS_OF_IMAGES // 2 - 1, 1) as turn:
                store_bias(turn * 2, 0)
                store_bias(turn * 2 + 1, 1)
            store_bias(GROUPS_OF_IMAGES - 2, 0)
            for r in range(2):
                sp.wait_ge(bias_stored[r], 16 * (GROUPS_OF_IMAGES // 2 - r))
            for p in range(2, AHEAD_PAIRS):
                sp.wait_ge(S["score_mm"], p - 1)
                load_bias(p, p % 2)
            store_bias(GROUPS_OF_IMAGES - 1, 1)
            for r in range(2):
                sp.wait_ge(bias_stored[r], 16 * (GROUPS_OF_IMAGES // 2))

            pieces = PAIRS // 2
            w1_piece = EXPERTS * W1_COLS // pieces
            w2_piece = EXPERTS * HID // pieces

            def load_weights(k):
                sp.dma_start(w1[:, ds(k * w1_piece, w1_piece)], w1_dram[:, ds(k * w1_piece, w1_piece)]).then_inc(S["w1_loaded"], 16)
                sp.dma_start(w2[:, ds(k * w2_piece, w2_piece)], w2_dram[:, ds(k * w2_piece, w2_piece)]).then_inc(S["w2_loaded"], 16)

            with sp.Fori(AHEAD_PAIRS // 2, PAIRS // 2, 1) as turn:
                p = turn * 2
                for r in range(2):
                    sp.wait_ge(S["score_mm"], p + r - 1)
                    load_bias(p + r, r)
                load_weights(turn - AHEAD_PAIRS // 2)
            for k in range(pieces - AHEAD_PAIRS // 2, pieces):
                load_weights(k)
            per_store = -(-TILES // XN_STORES)
            for k in range(XN_STORES):
                a, b = k * per_store, min(TILES, (k + 1) * per_store)
                sp.wait_ge(S["xn_kept"], b)
                sp.dma_start(xn_dram[a * P:b * P].rearrange("(i p) d -> p i d", p=P), xn_row[:, a:b]
                             ).then_inc(S["xn_stored"], 16)
            with sp.Fori(0, EXPERT_TILES // RING, 1) as turn:
                j = turn * RING
                for r in range(RING):
                    sp.wait_ge(S["y_done"], j + r + 1 + 2)
                    sp.dma_start(y_dram[ds((j + r) * P, P)], y_sb[:, r]).then_inc(y_stored[r], 16)
            rows = out.rearrange("b s d -> (b s) d")
            with sp.Fori(0, (TILES - 1) // 2, 1) as turn:
                i = turn * 2
                for r in range(2):
                    sp.wait_ge(S["acc_done"], i + r + 1)
                    sp.dma_start(rows[ds((i + r) * P, P)], acc[:, r]).then_inc(out_stored[r], 16)
            sp.wait_ge(S["acc_done"], TILES)
            sp.dma_start(rows[(TILES - 1) * P:T], acc[0:LAST, 0]).then_inc(out_stored[0], 16)
            sp.wait_ge(out_stored[0], 16 * (TILES // 2 + 1))
            sp.wait_ge(out_stored[1], 16 * (TILES // 2))

        @block.gpsimd
        def _(pool):
            g = nc.gpsimd
            g.memset(ident[:, :], 0.0)
            g.memset(not_earlier[:, :], -1.0)
            g.memset(tok_val[:, :], 0.0)
            g.memset(average[:, :], 1.0 / D).then_inc(S["pool_step"], 1)
            pool.wait_ge(S["pool_step"], 1)
            g.affine_select(out=ident[:, :], in_=ident[:, :], compare_op=ALU.not_equal, fill=1.0, base=0,
                            pattern=[[-1, P]], channel_multiplier=1).then_inc(S["pool_step"], 1)
            g.affine_select(out=not_earlier[:, :], in_=not_earlier[:, :], compare_op=ALU.is_ge, fill=0.0, base=0,
                            pattern=[[-1, P]], channel_multiplier=1)
            pool.wait_ge(S["pool_step"], 2)
            g.tensor_scalar(center[:, :], ident[:, :], 1.0 / D, None, ALU.subtract)
            g.memset(ones_b[:, :], 1.0)
            g.memset(ones_f[:, :], 1.0)
            g.memset(ctx_sb[:, :], 0.0)
            g.memset(eps[:, :], EPS)
            g.memset(zero[:, :], 0.0)
            g.memset(xs.rearrange("p r a t -> p (r a t)"), 0.0)
            g.memset(qs.rearrange("p r a t -> p (r a t)"), 0.0)
            g.memset(e_sb.rearrange("p r h s -> p (r h s)"), 0.0)
            g.iota(iota8[:, :], pattern=[[1, NE]], base=0, channel_multiplier=0, allow_small_or_imprecise_dtypes=True)
            g.iota(tile_no[:, :], pattern=[[P, 2]], base=0, channel_multiplier=1, allow_small_or_imprecise_dtypes=True)
            g.iota(tok_val[:, 0:TILES - 1], pattern=[[P, TILES - 1]], base=-MID, channel_multiplier=1,
                   allow_small_or_imprecise_dtypes=True)
            g.iota(tok_val[0:LAST, TILES - 1:TILES], pattern=[[P, 1]], base=(TILES - 1) * P - MID, channel_multiplier=1,
                   allow_small_or_imprecise_dtypes=True).then_inc(S["consts_made"], 1)

            nothing = zero[0:HEADS, 0:1].to_broadcast([HEADS, GT])

            def split(i, r, known, n):
                def part(k):
                    return bias_parts[:, r, k]
                if past(known, 2):
                    pool.wait_ge(bias_stored[r], (i - r) * 8)
                pool.wait_ge(S["bias_scaled"], i + 1)
                g.tensor_tensor(part(0), cb_f[:, r], nothing, ALU.add).then_inc(S["high_done"], 1)
                pool.wait_ge(S["high_done"], i + 1)
                g.tensor_tensor(cb_r, cb_f[:, r], part(0), ALU.subtract).then_inc(S["high_left"], 1)
                pool.wait_ge(S["high_left"], i + 1)
                g.tensor_tensor(part(1), cb_r, nothing, ALU.add).then_inc(S["middle_done"], 1)
                pool.wait_ge(S["middle_done"], i + 1)
                g.tensor_tensor(cb_m, cb_r, part(1), ALU.subtract).then_inc(S["middle_left"], 1)
                pool.wait_ge(S["middle_left"], i + 1)
                g.tensor_tensor(part(2), cb_m, nothing, ALU.add).then_inc(S["bias_split"], 1)
                if known == 0:
                    pool.wait_ge(S["k_done"], 1 + 2)
                    for p in range(2):
                        mix_keys(p, p)
                        copy_x(p, p)

            def mix_keys(p, r):
                keys = kT[:, ds(p * PT, PT)].rearrange("p (a s) -> p a s", a=2)
                mix = wp[:, C_MIX:C_MIX + HEADS].unsqueeze(1).unsqueeze(3)
                g.tensor_tensor(km[:, r].rearrange("p a (h s) -> p a h s", h=HEADS),
                                keys.unsqueeze(2).to_broadcast([P, 2, HEADS, TOK]),
                                mix.to_broadcast([P, 2, HEADS, TOK]), ALU.mult).then_inc(S["km_done"], 1)

            def copy_x(p, r):
                g.tensor_copy(xs[:, r].rearrange("p a (o t) -> p a o t", o=2)[:, :, :, 0:TOK],
                              xnT[:, ds(p * PT, PT)].rearrange("p (a t) -> p a t", a=2).unsqueeze(2)
                              .to_broadcast([P, 2, 2, TOK])).then_inc(S["xs_copied"], 1)

            def attend(p, r, known, n):
                pool.wait_ge(S["score_mm"], p + 1)
                if past(known, 2):
                    copy_x(p, r)
                if known is None or known + 2 < n:
                    mix_keys(p + 2, r)

            steps(pool, GROUPS_OF_IMAGES - 1, 0, split)
            for p in range(2):
                attend(p, p, p, PAIRS)
            split(GROUPS_OF_IMAGES - 1, (GROUPS_OF_IMAGES - 1) % 2, GROUPS_OF_IMAGES - 1, GROUPS_OF_IMAGES)
            steps(pool, PAIRS, 0, attend, ahead=2, done=2)

            def keep(i, r, known, n):
                pool.wait_ge(S["xn_rowed"], i + 2)
                g.tensor_copy(xn_row[:, ds(i, 1)].rearrange("p i d -> p (i d)"), xn_now[:, r]).then_inc(S["xn_kept"], 1)
            steps(pool, TILES, 0, keep)

            pool.wait_ge(S["logit_done"], TILES + 3)
            pool.wait_ge(S["xn_kept"], TILES)
            g.iota(iota_slot[:, :, :], pattern=[[1, P], [0, PICKS]], base=0, channel_multiplier=0,
                   allow_small_or_imprecise_dtypes=True)
            g.iota(iota_tile[:, :, :], pattern=[[1, EXPERT_TILES], [0, PICKS]], base=0, channel_multiplier=0,
                   allow_small_or_imprecise_dtypes=True)
            g.memset(not_first[:, :, 0:1], 0.0)
            g.memset(not_first[:, :, 1:TILES], 1.0).then_inc(S["tables_made"], 1)
            pool.wait_ge(S["groups_ready"], 1)
            g.tensor_tensor(prod_b, logits[:, :, NG:NG + EXPERTS].rearrange("p i (g e) -> p i g e", g=NG),
                            oh1[1].unsqueeze(3).to_broadcast([P, TILES, NG, NE]), ALU.mult
                            ).then_inc(S["product_b_done"], 1)
            pool.wait_ge(S["share_ready"], 1)
            n_c = [0]

            def link(ins):
                n_c[0] += 1
                ins.then_inc(S["step_c"], 1)
                pool.wait_ge(S["step_c"], n_c[0])

            def bc(a, shape):
                return a.to_broadcast(shape)

            sh2 = [share[:, 1, b, :].rearrange("p (i a) -> p i a", a=2).unsqueeze(3) for b in range(2)]
            link(g.tensor_tensor(sel, oh2[0], bc(sh2[0], [P, TILES, 2, NE]), ALU.mult))
            link(g.tensor_tensor(tmp_x, oh2[1], bc(sh2[1], [P, TILES, 2, NE]), ALU.mult))
            link(g.tensor_tensor(sel, sel, tmp_x, ALU.add))
            for a in range(2):
                sh1 = share[:, 0, a, 0:TILES].unsqueeze(2)
                link(g.tensor_tensor(sel[:, :, a], sel[:, :, a], bc(sh1, [P, TILES, NE]), ALU.mult))
            call = c_all.rearrange("p i (g e) -> p i g e", g=NG)
            link(g.tensor_tensor(call, bc(oh1[0].unsqueeze(3), [P, TILES, NG, NE]),
                                 bc(sel[:, :, 0].unsqueeze(2), [P, TILES, NG, NE]), ALU.mult))
            link(g.tensor_tensor(prod_b, bc(oh1[1].unsqueeze(3), [P, TILES, NG, NE]),
                                 bc(sel[:, :, 1].unsqueeze(2), [P, TILES, NG, NE]), ALU.mult))
            g.tensor_tensor(call, call, prod_b, ALU.add).then_inc(S["c_ready"], 1)

            pool.wait_ge(S["xn_stored"], 16 * XN_STORES)

            def gather(j, first, again):
                copied = (j + first) // GATHERS + 1 if not again else pool.to_reg(j * (RING // GATHERS) + first // GATHERS + 1)
                pool.wait_ge(S["table_done"], 1)
                pool.wait_ge(S["idx_copied"], copied)
                for r in range(first, first + GATHERS):
                    g.indirect_dma_start(xg[:, r], None, xn_dram, bass.IndirectOffsetOnAxis(idx_now[:, r:r + 1], 0)
                                         ).then_inc(gathered[r], 16)
            for first in range(0, RING, GATHERS):
                gather(0, first, False)
            with pool.Fori(1, EXPERT_TILES // RING, 1) as turn:
                for first in range(0, RING, GATHERS):
                    gather(turn, first, True)

            for r in range(RING):
                pool.wait_ge(y_stored[r], 16 * (EXPERT_TILES // RING))

            def fetch(i, r, again):
                copied = i + 1 if not again else pool.to_reg(i + 1)
                pool.wait_ge(S["table_done"], 1)
                pool.wait_ge(S["pos_copied"], copied)
                for k in range(PICKS):
                    g.indirect_dma_start(y_got[:, r, k], None, y_dram,
                                         bass.IndirectOffsetOnAxis(pos_now[:, r, k:k + 1], 0)).then_inc(y_fetched[r], 16)
            fetch(0, 0, False)
            fetch(1, 1, False)
            with pool.Fori(1, (TILES - 1) // 2, 1) as turn:
                i = turn * 2
                fetch(i, 0, True)
                fetch(i + 1, 1, True)
            fetch(TILES - 1, 0, True)

        @block.scalar
        def _(act):
            s = nc.scalar
            act.wait_ge(S["embed_loaded"], 16)
            act.wait_ge(S["consts_made"], 1)

            ahead_by_lag(act, {"spread_done": 1, "q_done": 2, "k_done": 2})

            def embed(i, r, known, n):
                if live(known, 0, n):
                    act.wait_ge(S["embed_mm"], i + 1)
                    s.activation(hT[:, ds(i * GT, GT)].rearrange("p (b t) -> p b t", t=TOK)[:, :, 1:TOK],
                                 bank[0][:, 0:GP].rearrange("p (b t) -> p b t", t=PATCHES), ACT.Identity,
                                 bias=wp[:, C_TOKB:C_TOKB + 1]).then_inc(S["h_placed"], 1)
                if live(known, 1, n):
                    act.wait_ge(S["var_mm"], i + 1)
                    s.activation(spread[:, 1 - r], bank[3][:, 0:GT], ACT.Sqrt, bias=eps[:, :]).then_inc(S["spread_done"], 1)
                if live(known, 2, n):
                    act.wait_ge(S["qk_mm"], i + 1)
                    s.activation(qT[:, ds((i - 2) * GT, GT)], bank[4][:, 0:GT], ACT.Copy, scale=SCALE
                                 ).then_inc(S["q_done"], 1)
                    s.activation(kT[:, ds((i - 2) * GT, GT)], bank[5][:, 0:GT], ACT.Copy).then_inc(S["k_done"], 1)
                    if past(known, 4):
                        act.wait_ge(S["bias_split"], i - 3)
                    s.activation(cb_f[:, r], bank[6 + r][0:HEADS, 0:GT], ACT.Copy, scale=SCALE).then_inc(S["bias_scaled"], 1)
                if live(known, 0, n):
                    act.wait_ge(S["center_mm"], i + 1)
                    s.activation(squares, bank[1 + r][:, 0:GT], ACT.Square).then_inc(S["squared"], 1)
            steps(act, GROUPS_OF_IMAGES, 2, embed)

            ahead_by_lag(act, {"v_done": 1, "pT_done": 1, "ctxT_done": 3})

            def attend(p, r, known, n):
                if live(known, 3, n):
                    act.wait_ge(S["context_turned"], p + 1)
                    s.activation(ctxT[:, :].rearrange("p (a t) -> p a t", a=2),
                                 bank[6][:, 0:P].rearrange("p (a t) -> p a t", a=2)[:, :, 0:TOK], ACT.Copy
                                 ).then_inc(S["ctxT_done"], 1)
                if live(known, 1, n):
                    act.wait_ge(S["v_mm"], p + 1)
                    s.activation(v_sb[:, 1 - r], bank[2][:, 0:2 * D].rearrange("p (a d) -> p a d", a=2), ACT.Copy
                                 ).then_inc(S["v_done"], 1)
                    act.wait_ge(S["exps_turned"], p + 1)
                    s.activation(pT[:, 1 - r],
                                 bank[3][:, :].rearrange("p (h a t) -> p h a t", h=4, a=2)[:, :, :, 0:TOK],
                                 ACT.Copy).then_inc(S["pT_done"], 1)
                if live(known, 0, n):
                    act.wait_ge(S["lessened"], p + 1)
                    s.activation(e_sb[:, r, :, 0:TOK], e_sb[:, r, :, 0:TOK], ACT.Exp).then_inc(S["exped"], 1)
            steps(act, PAIRS, 3, attend)

            act.wait_ge(S["h_added"], PAIRS + 3)
            ahead_by_lag(act, {"sd_done": 1, "xnT_done": 2, "logit_done": 3})

            def rows(i, r, known, n):
                if live(known, 0, n):
                    act.wait_ge(S["h_turned"], i + 1)
                    s.activation(h_tok[:, ds(i, 1)].rearrange("p i d -> p (i d)"), bank[r][:, 0:P], ACT.Copy
                                 ).then_inc(S["h_rowed"], 1)
                if live(known, 1, n):
                    act.wait_ge(S["moments_done"], i)
                    s.activation(sd2[:, 1 - r:2 - r], moments[:, 1 - r, 1:2], ACT.Sqrt, bias=eps[:, :]
                                 ).then_inc(S["sd_done"], 1)
                if live(known, 3, n):
                    act.wait_ge(S["logit_mm"], i + 1)
                    s.activation(logits[:, ds(i - 3, 1)].rearrange("p i e -> p (i e)"),
                                 bank[5 - r][:, 0:NG + EXPERTS], ACT.Copy).then_inc(S["logit_done"], 1)
                if live(known, 2, n):
                    act.wait_ge(S["xn_turned"], i + 1)
                    s.activation(xnT2[:, r], bank[2 + r][:, 0:P], ACT.Copy).then_inc(S["xnT_done"], 1)
            steps(act, TILES, 3, rows)

            act.wait_ge(S["gap_ready"], 1)
            s.activation(egap, gap, ACT.Exp).then_inc(S["exp_ready"], 1)

            act.wait_ge(S["c_ready"], 1)

            def weight_tiles(i, r, known, n):
                if past(known, 2):
                    act.wait_ge(S["table_mm"], i - 1)
                act.wait_ge(S["tiles_onehot"], i + 1)
                s.activation(onehot_tok[:, r], onehot_tile[:, r], ACT.Copy, scale=tok_val[:, ds(i, 1)]
                             ).then_inc(S["weighted_done"], 1)
            steps(act, TILES, 0, weight_tiles)

            act.wait_ge(S["tiles_known"], 1)

            ahead_by_lag(act, {"relu_done": 1, "y_done": 2})

            def expert(j, known, slot, turn):
                n = EXPERT_TILES
                if live(known, 1, n):
                    before = (slot - 1) % 2
                    act.wait_ge(S["hidden_mm"], j + 1)
                    for half in range(2):
                        last = s.activation(hidT[:, before, half], bank[2 + before][:, half * P:half * P + P], ACT.Relu,
                                            bias=w1_now[:, before, HID + half:HID + half + 1])
                    last.then_inc(S["relu_done"], 1)
                if live(known, 2, n):
                    back = (slot - 2) % RING
                    if past(known, RING + 2):
                        act.wait_ge(y_stored[back], 16 * (turn if slot >= 2 else turn - 1))
                    act.wait_ge(S["y_mm"], j + 1)
                    s.activation(y_sb[:, back], bank[4 + slot % 2][:, 0:D], ACT.Copy).then_inc(S["y_done"], 1)
            expert_steps(act, 2, 2, expert)

            act.wait_ge(S["c_ready"], 1)
            for r in range(RING):
                act.wait_ge(y_stored[r], 16 * (EXPERT_TILES // RING))

            def biases(i, r, known, n):
                if live(known, 0, n):
                    if past(known, 2):
                        act.wait_ge(S["c_turned"], i - 1)
                    s.activation(c_now[:, r], c_all[:, ds(i, 1)].to_broadcast([P, 2, EXPERTS]), ACT.Copy
                                 ).then_inc(S["c_copied"], 1)
                    act.wait_ge(S["c_turned"], i + 1)
                    if past(known, 2):
                        act.wait_ge(S["b2_mm"], i - 1)
                    s.activation(cT[:, r], bank[r][0:EXPERTS, 0:P], ACT.Copy).then_inc(S["cT_done"], 1)
            steps(act, TILES, 0, biases)

        @block.tensor
        def _(pe):
            t = nc.tensor
            pe.wait_ge(S["embed_loaded"], 16)
            pe.wait_ge(S["consts_made"], 1)

            ahead_by_lag(pe, {"var_mm": 1, "qk_mm": 2})
            pe.wait_ge(S["cls_placed"], 1)

            def embed(i, r, known, n):
                if live(known, 0, n):
                    pe.wait_ge(x_loaded[r], (i - r) * 8 + 16)
                    for c in range(K_CHUNKS):
                        last = t.matmul(bank[0][:, 0:GP], wp[:, C_TOKW + c * P:C_TOKW + (c + 1) * P],
                                        x_sb[:, ds(i, 1), c].rearrange("p g n -> p (g n)"),
                                        start=(c == 0), stop=(c == K_CHUNKS - 1))
                    last.then_inc(S["embed_mm"], 1)
                if live(known, 1, n):
                    pe.wait_ge(S["squared"], i)
                    t.matmul(bank[3][:, 0:GT], average[:, :], squares, start=True, stop=True).then_inc(S["var_mm"], 1)
                if known == 2:
                    pe.wait_ge(S["small_loaded"], 16)
                if live(known, 2, n):
                    pe.wait_ge(S["xn_done"], i)
                    if not live(known, 1, n):
                        pe.wait_ge(S["k_done"], i)
                    xn = xnT[:, ds((i - 2) * GT, GT)]
                    t.matmul(bank[4][:, 0:GT], wp[:, C_Q:C_Q + D], xn, start=True, stop=True)
                    t.matmul(bank[5][:, 0:GT], wp[:, C_K:C_K + D], xn, start=True, stop=True)
                    t.matmul(bank[6 + r][0:HEADS, 0:GT], wp[:, C_B:C_B + HEADS], xn, start=True, stop=True
                             ).then_inc(S["qk_mm"], 1)
                if live(known, 0, n):
                    pe.wait_ge(S["h_placed"], i + 1)
                    t.matmul(bank[1 + r][:, 0:GT], center[:, :], hT[:, ds(i * GT, GT)], start=True, stop=True
                             ).then_inc(S["center_mm"], 1)
            steps(pe, GROUPS_OF_IMAGES, 2, embed)
            pe.wait_ge(S["q_done"], GROUPS_OF_IMAGES + 2)
            pe.wait_ge(S["k_done"], GROUPS_OF_IMAGES + 2)

            ahead_by_lag(pe, {"v_mm": 1, "exps_turned": 1, "context_mm": 2, "context_turned": 3, "project_mm": 3})

            def attend(p, r, known, n):
                if live(known, 0, n):
                    pe.wait_ge(S["qs_copied"], p + 1)
                    pe.wait_ge(S["km_done"], p + 1)
                    pe.wait_ge(bias_loaded[r], (p - r) * 8 + 16)
                    for a in range(2):
                        scores = bank[r][64 * a:64 * a + 64, 0:HS]
                        t.matmul(scores, qs[:, r, a], km[:, r, a], start=True, stop=False)
                        last = t.matmul(scores, ones_b[0:SPLITS, 0:64],
                                        bias_row[:, r].rearrange("s (h a t) -> s h a t", h=HEADS, a=2)[:, :, a],
                                        start=False, stop=True)
                    last.then_inc(S["score_mm"], 1)
                if live(known, 3, n):
                    pe.wait_ge(S["ctx_copied"], p)
                    t.transpose(bank[6][:, 0:P], ctx_sb[:, :], ident[:, :]).then_inc(S["context_turned"], 1)
                if live(known, 2, n):
                    pe.wait_ge(S["pT_done"], p)
                if live(known, 1, n):
                    pe.wait_ge(S["xs_copied"], p)
                    for a in range(2):
                        last = t.matmul(bank[2][:, a * D:(a + 1) * D], xs[:, 1 - r, a],
                                        wp[:, C_V:C_V + D], start=True, stop=True)
                    last.then_inc(S["v_mm"], 1)
                    pe.wait_ge(S["exped"], p)
                    for h in range(0, HEADS, 2):
                        last = t.transpose(bank[3][:, h * 64:h * 64 + P],
                                           e_sb[:, 1 - r, h:h + 2].rearrange("p h s -> p (h s)"), ident[:, :])
                    last.then_inc(S["exps_turned"], 1)
                if live(known, 3, n):
                    if past(known, 4):
                        pe.wait_ge(S["h_added"], p)
                    pe.wait_ge(S["ctxT_done"], p + 1)
                    t.matmul(bank[7][:, 0:PT], wp[:, C_D:C_D + D], ctxT[:, :], start=True, stop=True
                             ).then_inc(S["project_mm"], 1)
                if live(known, 2, n):
                    for a in range(2):
                        for h in range(HEADS):
                            o = 64 * (h % 2)
                            last = t.matmul(bank[4 + h % 2][64 * a:64 * a + TOK, (h // 2) * DH:(h // 2 + 1) * DH],
                                            pT[o:o + TOK, r, h // 2, a],
                                            v_sb[o:o + TOK, r, a, h * DH:(h + 1) * DH], start=True, stop=True)
                    last.then_inc(S["context_mm"], 1)
            steps(pe, PAIRS, 3, attend, turn=4)

            ahead_by_lag(pe, {"xn_turned": 2, "logit_mm": 3})

            def rows(i, r, known, n):
                if live(known, 0, n):
                    pe.wait_ge(S["hs_copied"], i + 1)
                    if past(known, 2):
                        pe.wait_ge(S["h_rowed"], i - 1)
                    t.transpose(bank[r][:, 0:P], hs[:, r], ident[:, :]).then_inc(S["h_turned"], 1)
                if live(known, 3, n):
                    pe.wait_ge(S["xnT_done"], i)
                    t.matmul(bank[5 - r][:, 0:NG + EXPERTS], xnT2[:, 1 - r], wp[:, C_R:C_R + NG + EXPERTS],
                             start=True, stop=True).then_inc(S["logit_mm"], 1)
                if live(known, 2, n):
                    pe.wait_ge(S["xn_rowed"], i)
                    t.transpose(bank[2 + r][:, 0:P], xn_now[:, r], ident[:, :]).then_inc(S["xn_turned"], 1)
            steps(pe, TILES, 3, rows)

            pe.wait_ge(S["mask_ready"], 1)
            t.matmul(bank[5][:, 0:EXPERTS], ones_b[:, :], seen_sum[:, :, TILES - 1], start=True, stop=True
                     ).then_inc(S["totals_mm"], 1)
            per = 512 // EXPERTS
            blocks = [(k, k * per, min(TILES, (k + 1) * per)) for k in range(-(-TILES // per))]
            for k, a, b in blocks:
                rank = bank[k][:, 0:(b - a) * EXPERTS]
                t.matmul(rank, ones_b[:, :], seen_sum[:, :, a:b].rearrange("p e i -> p i e"), start=True, stop=False)
                t.matmul(rank, not_earlier[:, :], seen[:, :, a:b].rearrange("p e i -> p i e"), start=False, stop=False)
            pe.wait_ge(S["starts_ready"], 1)
            for k, a, b in blocks:
                last = t.matmul(bank[k][:, 0:(b - a) * EXPERTS], ones_b[:, :],
                                tiles_start.unsqueeze(1).to_broadcast([P, b - a, EXPERTS]), start=False, stop=True)
            last.then_inc(S["rank_mm"], 1)
            pe.wait_ge(S["ecol_ready"], 1)
            for c in range(2):
                last = t.matmul(bank[3][0:1, c * P:(c + 1) * P], e_col[:, c:c + 1], ident[:, :], start=True, stop=True)
            last.then_inc(S["erow_mm"], 1)

            def table(i, r, known, n):
                pe.wait_ge(S["slots_onehot"], i + 1)
                pe.wait_ge(S["weighted_done"], i + 1)
                for k in range(PICKS):
                    last = t.matmul(bank[4][:, 0:EXPERT_TILES], onehot_slot[:, r, :, k], onehot_tok[:, r, :, k],
                                    start=(known == 0 and k == 0), stop=(known == n - 1 and k == PICKS - 1),
                                    skip_group_check=True)
                last.then_inc(S["table_mm"], 1)
            steps(pe, TILES, 0, table)

            pe.wait_ge(S["w1_loaded"], 16 * (PAIRS // 2))
            pe.wait_ge(S["w2_loaded"], 16 * (PAIRS // 2))
            pe.wait_ge(S["tiles_known"], 1)
            pe.wait_ge(S["table_done"], 1)

            ahead_by_lag(pe, {"hidden_mm": 1, "y_mm": 2})

            def expert(j, known, slot, turn):
                n = EXPERT_TILES
                if live(known, 0, n):
                    pe.wait_ge(gathered[slot], turn * 16 + 16)
                    t.transpose(bank[slot % 2][:, 0:P], xg[:, slot], ident[:, :]).then_inc(S["x_turned"], 1)
                if live(known, 1, n):
                    before = (slot - 1) % 2
                    pe.wait_ge(S["x_ready"], j)
                    for half in range(2):
                        last = t.matmul(bank[2 + before][:, half * P:half * P + P],
                                        w1_now[:, before, half * P:half * P + P], xgT[:, before], start=True, stop=True)
                    last.then_inc(S["hidden_mm"], 1)
                if live(known, 2, n):
                    e = expert_of(pe, j - 2)
                    pe.wait_ge(S["relu_done"], j)
                    for half in range(2):
                        last = t.matmul(bank[4 + slot % 2][:, 0:D], hidT[:, slot % 2, half],
                                        w2[:, ds(e * HID + half * D, D)], start=(half == 0), stop=(half == 1))
                    last.then_inc(S["y_mm"], 1)
            expert_steps(pe, 2, 1, expert)

            pe.wait_ge(S["b2_loaded"], 16)

            def biases(i, r, known, n):
                pe.wait_ge(S["c_copied"], i + 1)
                if past(known, 2):
                    pe.wait_ge(S["cT_done"], i - 1)
                t.transpose(bank[r][:, 0:P], c_now[:, r].rearrange("p a e -> p (a e)"), ident[:, :]).then_inc(S["c_turned"], 1)
                pe.wait_ge(S["cT_done"], i + 1)
                if past(known, 2):
                    pe.wait_ge(S["base_done"], i - 1)
                t.matmul(bank[2 + r][:, 0:D], cT[:, r], b2[:, :], start=True, stop=True).then_inc(S["b2_mm"], 1)
            steps(pe, TILES, 0, biases)

        @block.vector
        def _(dve):
            v = nc.vector
            dve.wait_ge(S["embed_loaded"], 16)
            dve.wait_ge(S["consts_made"], 1)
            v.tensor_copy(hT[:, 0:T].rearrange("p (b t) -> p b t", t=TOK)[:, :, 0],
                          wp[:, C_CLS:C_CLS + 1].to_broadcast([P, IMAGES])).then_inc(S["cls_placed"], 1)
            v.memset(hT[:, T:TP], 0.0).then_inc(S["pads_done"], 1)

            ahead_by_lag(dve, {"inv_done": 1, "xn_done": 1})

            def embed(i, r, known, n):
                if live(known, 1, n):
                    dve.wait_ge(S["spread_done"], i + 1)
                    dve.wait_ge(S["xn_done"], i)
                    v.reciprocal(inv, spread[:, 1 - r]).then_inc(S["inv_done"], 1)
                    dve.wait_ge(S["inv_done"], i + 1)
                    v.tensor_tensor(xnT[:, ds((i - 1) * GT, GT)], bank[2 - r][:, 0:GT], inv, ALU.mult
                                    ).then_inc(S["xn_done"], 1)
            steps(dve, GROUPS_OF_IMAGES, 1, embed)
            dve.wait_ge(S["q_done"], GROUPS_OF_IMAGES + 2)
            dve.wait_ge(S["pads_done"], 1)

            def copies(p, r):
                v.tensor_copy(qs[:, r, :, 0:TOK], qT[:, ds(p * PT, PT)].rearrange("p (a t) -> p a t", a=2)
                              ).then_inc(S["qs_copied"], 1)


            copies(0, 0)
            ahead_by_lag(dve, {"summed": 1, "inverted": 1, "h_added": 3, "ctx_copied": 2})

            def attend(p, r, known, n):
                if live(known, 0, n):
                    if known is None or known + 1 < n:
                        copies(p + 1, 1 - r)
                    dve.wait_ge(S["score_mm"], p + 1)
                    sc = bank[r][:, 0:HS].rearrange("p (h s) -> p h s", h=HEADS)
                    e = e_sb[:, r, :, 0:TOK]
                    v.tensor_reduce(top[:, r], sc, AX.X, ALU.max).then_inc(S["maxed"], 1)
                if live(known, 1, n):
                    dve.wait_ge(S["exped"], p)
                    v.tensor_reduce(total[:, 1 - r], e_sb[:, 1 - r, :, 0:TOK], AX.X, ALU.add).then_inc(S["summed"], 1)
                if live(known, 0, n):
                    dve.wait_ge(S["maxed"], p + 1)
                    v.tensor_tensor(e, sc, top[:, r].unsqueeze(2).to_broadcast([P, HEADS, TOK]), ALU.subtract
                                    ).then_inc(S["lessened"], 1)
                if live(known, 1, n):
                    dve.wait_ge(S["summed"], p + 1)
                    if past(known, 3):
                        dve.wait_ge(S["ctx_copied"], p)
                    v.reciprocal(inv_total[:, 1 - r], total[:, 1 - r]).then_inc(S["inverted"], 1)
                if live(known, 2, n):
                    dve.wait_ge(S["inverted"], p)
                    dve.wait_ge(S["context_mm"], p + 1)
                    for o in range(2):
                        last = v.tensor_tensor(
                            ctx_sb[:, :].rearrange("p (h o d) -> p h o d", o=2, d=DH)[:, :, o],
                            bank[4 + o][:, 0:D // 2].rearrange("p (h d) -> p h d", d=DH),
                            inv_total[:, r].rearrange("p (h o) -> p h o", o=2)[:, :, o].unsqueeze(2)
                            .to_broadcast([P, HEADS // 2, DH]), ALU.mult)
                    last.then_inc(S["ctx_copied"], 1)
                if live(known, 3, n):
                    dve.wait_ge(S["project_mm"], p + 1)
                    hp = hT[:, ds((p - 3) * PT, PT)]
                    v.scalar_tensor_tensor(out=hp, in0=bank[7][:, 0:PT], scalar=wp[:, C_BD:C_BD + 1], in1=hp,
                                           op0=ALU.add, op1=ALU.add).then_inc(S["h_added"], 1)
            steps(dve, PAIRS, 3, attend, ahead=1)

            dve.wait_ge(S["h_added"], PAIRS + 3)

            def copy_h(i, r):
                v.tensor_copy(hs[:, r], hT[:, ds(i * P, P)]).then_inc(S["hs_copied"], 1)
            copy_h(0, 0)
            copy_h(1, 1)
            ahead_by_lag(dve, {"rstd_done": 1, "xn_rowed": 1})

            def rows(i, r, known, n):
                if live(known, 0, n):
                    dve.wait_ge(S["h_rowed"], i + 1)
                    v.bn_stats(stats[:, r], h_tok[:, ds(i, 1)].rearrange("p i d -> p (i d)")).then_inc(S["stat_done"], 1)
                    dve.wait_ge(S["stat_done"], i + 1)
                if live(known, 1, n):
                    dve.wait_ge(S["sd_done"], i + 1)
                    v.reciprocal(rstd2[:, 1 - r:2 - r], sd2[:, 1 - r:2 - r]).then_inc(S["rstd_done"], 1)
                if known is None or known + 2 < n:
                    copy_h(i + 2, r)
                if live(known, 0, n):
                    v.bn_aggr(moments[:, r], stats[:, r]).then_inc(S["moments_done"], 1)
                if live(known, 1, n):
                    dve.wait_ge(S["rstd_done"], i + 1)
                    if past(known, 3):
                        dve.wait_ge(S["xn_kept"], i - 2)
                    if not live(known, 0, n):
                        dve.wait_ge(S["xn_turned"], i)
                    v.tensor_scalar(xn_now[:, 1 - r], h_tok[:, ds(i - 1, 1)].rearrange("p i d -> p (i d)"),
                                    moments[:, 1 - r, 0:1], rstd2[:, 1 - r:2 - r], ALU.subtract, ALU.mult
                                    ).then_inc(S["xn_rowed"], 1)
            steps(dve, TILES, 1, rows, ahead=2, turn=4)

            n_r = [0]

            def link(ins):
                n_r[0] += 1
                ins.then_inc(S["route"], 1)
                dve.wait_ge(S["route"], n_r[0])

            dve.wait_ge(S["logit_done"], TILES + 3)
            dve.wait_ge(S["xn_kept"], TILES)

            def top2(x, n, best_a, best_b, hot_a, hot_b, signal=None):
                def wide(a):
                    return a.unsqueeze(2).to_broadcast([P, n, NE])
                idx = tmp_i.rearrange("p i a e -> p (i a) e")[:, 0:n]
                rest = tmp_x.rearrange("p i a e -> p (i a) e")[:, 0:n]
                iota = iota8[:, :].unsqueeze(1).to_broadcast([P, n, NE])
                for m, hot in ((best_a, hot_a), (best_b, hot_b)):
                    link(v.tensor_reduce(m, x, AX.X, ALU.max))
                    link(v.tensor_tensor(idx, x, wide(m), ALU.is_equal))
                    link(v.scalar_tensor_tensor(out=idx, in0=idx, scalar=-float(NE), in1=iota, op0=ALU.mult, op1=ALU.add))
                    link(v.tensor_reduce(lowest[:, 0:n], idx, AX.X, ALU.min))
                    ins = v.tensor_tensor(hot, idx, wide(lowest[:, 0:n]), ALU.is_equal)
                    if hot is hot_b and signal:
                        ins.then_inc(S[signal], 1)
                        dve.wait_ge(S[signal], 1)
                    else:
                        link(ins)
                    if m is best_a:
                        link(v.scalar_tensor_tensor(out=rest, in0=hot, scalar=LOW, in1=x, op0=ALU.mult, op1=ALU.add))
                        x = rest

            l1 = logits[:, :, 0:NG]
            l2 = logits[:, :, NG:NG + EXPERTS].rearrange("p i (g e) -> p i g e", g=NG)
            top2(l1, TILES, best[:, 0, 0, 0:TILES], best[:, 0, 1, 0:TILES], oh1[0], oh1[1], "groups_ready")
            link(v.tensor_tensor(prod, l2, oh1[0].unsqueeze(3).to_broadcast([P, TILES, NG, NE]), ALU.mult))
            v.tensor_reduce(sel[:, :, 0], prod.rearrange("p i g e -> p i e g"), AX.X, ALU.add)
            dve.wait_ge(S["product_b_done"], 1)
            link(v.tensor_reduce(sel[:, :, 1], prod_b.rearrange("p i g e -> p i e g"), AX.X, ALU.add))
            flat = [x.rearrange("p i a e -> p (i a) e") for x in (sel, oh2[0], oh2[1])]
            top2(flat[0], 2 * TILES, best[:, 1, 0], best[:, 1, 1], flat[1], flat[2])
            v.tensor_tensor(tmp_x, oh2[0], oh2[1], ALU.add).then_inc(S["picked_ready"], 1)
            v.memset(gap[:, 0, TILES:2 * TILES], 0.0)
            v.tensor_tensor(gap[:, 0, 0:TILES], best[:, 0, 1, 0:TILES], best[:, 0, 0, 0:TILES], ALU.subtract)
            v.tensor_tensor(gap[:, 1], best[:, 1, 1], best[:, 1, 0], ALU.subtract).then_inc(S["gap_ready"], 1)
            dve.wait_ge(S["picked_ready"], 1)
            for a, out_ in ((0, seen), (1, seen_b)):
                last = v.tensor_tensor(
                    out_.rearrange("p (g e) i -> p g e i", g=NG),
                    oh1[a].rearrange("p i g -> p g i").unsqueeze(2).to_broadcast([P, NG, NE, TILES]),
                    tmp_x[:, :, a].rearrange("p i e -> p e i").unsqueeze(1).to_broadcast([P, NG, NE, TILES]), ALU.mult)
            link(last)
            link(v.tensor_tensor(seen, seen, seen_b, ALU.add))
            link(v.memset(seen[LAST:P, :, TILES - 1], 0.0))
            dve.wait_ge(S["tables_made"], 1)
            v.tensor_tensor_scan(seen_sum.rearrange("p e i -> p (e i)"), not_first.rearrange("p e i -> p (e i)"),
                                 seen.rearrange("p e i -> p (e i)"), 0.0, ALU.mult, ALU.add).then_inc(S["mask_ready"], 1)
            dve.wait_ge(S["exp_ready"], 1)
            link(v.tensor_scalar(den, egap, 1.0, None, ALU.add))
            link(v.reciprocal(share[:, :, 0], den))
            link(v.tensor_tensor(share[:, :, 1], egap, share[:, :, 0], ALU.mult))
            wk = weight.rearrange("p i (a b) -> p i a b", a=2)
            for a in range(2):
                for b in range(2):
                    sh2 = share[:, 1, b, :].rearrange("p (i a) -> p i a", a=2)[:, :, a]
                    last = v.tensor_tensor(wk[:, :, a, b], share[:, 0, a, 0:TILES], sh2, ALU.mult)
            link(last)
            v.memset(cmp, 0.0).then_inc(S["share_ready"], 1)

            dve.wait_ge(S["totals_mm"], 1)
            link(v.tensor_scalar(count_i, bank[5][:, 0:EXPERTS], float(P - 1), None, ALU.add))
            link(v.tensor_single_scalar(count_s, count_i, 7, ALU.arith_shift_right))
            link(v.tensor_copy(tiles_f, count_s))
            link(v.tensor_tensor_scan(tiles_end, ones_f[:, :], tiles_f, 0.0, ALU.mult, ALU.add))
            v.tensor_tensor(tiles_start, tiles_end, tiles_f, ALU.subtract).then_inc(S["starts_ready"], 1)
            for c in range(2):
                link(v.tensor_scalar(cmp, tiles_end, tile_no[:, c:c + 1], None, ALU.is_le))
                ins = v.tensor_reduce(e_col[:, c:c + 1], cmp, AX.X, ALU.add)
                if c == 0:
                    link(ins)
                else:
                    ins.then_inc(S["ecol_ready"], 1)
            dve.wait_ge(S["rank_mm"], 1)
            per = 512 // EXPERTS
            pos4 = pos_f.rearrange("p i (a b) -> p i a b", a=2)
            for a in range(2):
                for k in range(-(-TILES // per)):
                    i0, i1 = k * per, min(TILES, (k + 1) * per)
                    last = v.tensor_tensor(
                        prod[:, i0:i1], bank[k][:, 0:(i1 - i0) * EXPERTS].rearrange("p (i g e) -> p i g e", g=NG, e=NE),
                        oh1[a][:, i0:i1].unsqueeze(3).to_broadcast([P, i1 - i0, NG, NE]), ALU.mult)
                link(last)
                link(v.tensor_reduce(tmp_i[:, :, a], prod.rearrange("p i g e -> p i e g"), AX.X, ALU.add))
            dve.wait_ge(S["step_c"], 3)
            for b in range(2):
                link(v.tensor_tensor(tmp_x, tmp_i, oh2[b], ALU.mult))
                link(v.tensor_reduce(pos4[:, :, :, b], tmp_x, AX.X, ALU.add))
            link(v.tensor_scalar(pos_f, pos_f, float(SLOTS - 1), None, ALU.min))
            link(v.tensor_copy(pos_i, pos_f))
            link(v.tensor_single_scalar(hi_i, pos_i, 7, ALU.arith_shift_right))
            link(v.tensor_copy(hi_h, hi_i))
            link(v.scalar_tensor_tensor(out=lo_h, in0=hi_h, scalar=-float(P), in1=pos_f, op0=ALU.mult, op1=ALU.add))
            dve.wait_ge(S["erow_mm"], 1)
            v.tensor_scalar(tile_expert, bank[3][0:1, 0:2 * P], float(EXPERTS - 1), None, ALU.min
                            ).then_inc(S["tiles_known"], 1)

            def one_hots(i, r, known, n):
                for out_, iota, place, used_by, signal in (
                        (onehot_tile, iota_tile, hi_h, "weighted_done", "tiles_onehot"),
                        (onehot_slot, iota_slot, lo_h, "table_mm", "slots_onehot")):
                    if past(known, 2):
                        dve.wait_ge(S[used_by], i - 1)
                    mine = place[:, ds(i, 1)].rearrange("p i k -> p (i k)").unsqueeze(1)
                    v.tensor_tensor(out_[:, r], iota, mine.to_broadcast(list(iota.shape)), ALU.is_equal
                                    ).then_inc(S[signal], 1)
            steps(dve, TILES, 0, one_hots, turn=4)
            dve.wait_ge(S["table_mm"], TILES)
            v.tensor_scalar(slot_token, bank[4][:, 0:EXPERT_TILES], float(MID), None, ALU.add
                            ).then_inc(S["table_done"], 1)
            dve.wait_ge(S["table_done"], 1)
            dve.wait_ge(S["c_ready"], 1)

            def idx_copy(j, slot):
                v.tensor_copy(idx_now[:, slot:slot + GATHERS], slot_token[:, ds(j, GATHERS)]).then_inc(S["idx_copied"], 1)

            for j in range(0, RING, GATHERS):
                idx_copy(j, j)

            def expert(j, known, slot, turn):
                e = expert_of(dve, j)
                dve.wait_ge(S["x_turned"], j + 1)
                v.tensor_copy(xgT[:, slot % 2], bank[slot % 2][:, 0:P])
                if past(known, 2):
                    dve.wait_ge(S["relu_done"], j)
                v.tensor_copy(w1_now[:, slot % 2], w1[:, ds(e * W1_COLS, W1_COLS)]).then_inc(S["x_ready"], 1)
                if slot % GATHERS == GATHERS - 1 and (known is None or known + RING < EXPERT_TILES):
                    first = slot - GATHERS + 1
                    idx_copy((turn + 1) * RING + first, first)

            for j in range(RING):
                expert(j, j, j, 0)
            with dve.Fori(1, EXPERT_TILES // RING - 1, 1) as turn:
                for slot in range(RING):
                    expert(turn * RING + slot, None, slot, turn)
            for slot in range(RING):
                expert(EXPERT_TILES - RING + slot, EXPERT_TILES - RING + slot, slot, EXPERT_TILES // RING - 1)

            for r in range(RING):
                dve.wait_ge(y_stored[r], 16 * (EXPERT_TILES // RING))

            def pos_copy(i, r):
                v.tensor_copy(pos_now[:, r], pos_i[:, ds(i, 1)].rearrange("p i k -> p (i k)")).then_inc(S["pos_copied"], 1)

            pos_copy(0, 0)
            pos_copy(1, 1)

            def combine(i, r, known, n):
                dve.wait_ge(S["b2_mm"], i + 1)
                if past(known, 2):
                    dve.wait_ge(out_stored[r], (i - r) * 8)
                v.tensor_tensor(acc[:, r], bank[2 + r][:, 0:D], h_tok[:, ds(i, 1)].rearrange("p i d -> p (i d)"), ALU.add
                                ).then_inc(S["base_done"], 1)
                dve.wait_ge(S["base_done"], i + 1)
                dve.wait_ge(y_fetched[r], (i - r) * 8 * PICKS + 16 * PICKS)
                for k in range(PICKS):
                    ins = v.scalar_tensor_tensor(out=acc[:, r], in0=y_got[:, r, k],
                                                 scalar=weight[:, ds(i, 1), k], in1=acc[:, r], op0=ALU.mult, op1=ALU.add)
                    if k < PICKS - 1:
                        ins.then_inc(S["acc_step"], 1)
                        dve.wait_ge(S["acc_step"], i * (PICKS - 1) + k + 1)
                    else:
                        ins.then_inc(S["acc_done"], 1)
                if known is None or known + 2 < n:
                    pos_copy(i + 2, r)
            for i in range(2):
                combine(i, i % 2, i, TILES)
            with dve.Fori(1, (TILES - 3) // 2, 1) as turn:
                i = turn * 2
                combine(i, 0, None, TILES)
                combine(i + 1, 1, None, TILES)
            for i in range(TILES - 3, TILES):
                combine(i, i % 2, i, TILES)


def kernel(x, cls_tok, L0_tok_w, L0_tok_b, L0_attn_Wq, L0_attn_Wk, L0_attn_Wv, L0_attn_Wb, L0_attn_mixing, L0_attn_Wd,
           L0_attn_bd, L0_ffn_g1, L0_ffn_g2, L0_ffn_W1, L0_ffn_b1, L0_ffn_W2, L0_ffn_b2):
    import numpy as np
    import concourse.bacc as bacc
    from concourse.bass_utils import run_bass_kernel_spmd

    a = np.asarray
    px = a(x).reshape(IMAGES, 3, 6, 16, 6, 16).transpose(1, 3, 5, 0, 2, 4).reshape(K_CHUNKS, P, GROUPS_OF_IMAGES, GP)
    px = px.transpose(2, 1, 0, 3)
    small = np.concatenate([
        a(L0_tok_w).T.reshape(K_CHUNKS, P, D).transpose(1, 0, 2).reshape(P, K_CHUNKS * D),
        a(L0_tok_b).reshape(D, 1), a(cls_tok).reshape(D, 1),
        a(L0_attn_Wq).T, a(L0_attn_Wk).T, a(L0_attn_Wv).T, a(L0_attn_Wd).T,
        a(L0_ffn_g1), a(L0_ffn_g2).transpose(1, 0, 2).reshape(D, EXPERTS),
        a(L0_attn_Wb).T, a(L0_attn_mixing).T,
        a(L0_attn_bd).reshape(D, 1)], axis=1)
    w1 = np.concatenate([a(L0_ffn_W1).reshape(EXPERTS, D, HID).transpose(1, 0, 2),
                         a(L0_ffn_b1).reshape(EXPERTS, 2, P).transpose(2, 0, 1)], axis=2).reshape(D, EXPERTS * W1_COLS)
    w2 = a(L0_ffn_W2).reshape(EXPERTS, 2, P, D).transpose(2, 0, 1, 3).reshape(P, EXPERTS * HID)
    b2 = a(L0_ffn_b2).reshape(EXPERTS, D)
    arrays = {"patches_in": px, "small_in": small, "w1_in": w1, "w2_in": w2, "b2_in": b2}
    arrays = {k: np.ascontiguousarray(v) for k, v in arrays.items()}

    nc = bacc.Bacc("TRN2", target_bir_lowering=False, num_devices=1)
    aps = [nc.dram_tensor(k, v.shape, mybir.dt.from_np(v.dtype), kind="ExternalInput").ap() for k, v in arrays.items()]
    out = nc.dram_tensor("out", [IMAGES, TOK, D], F32, kind="ExternalOutput").ap()
    build(nc, *aps, out)
    r = run_bass_kernel_spmd(nc, [arrays], core_ids=[0])
    return r.results[0]["out"]
```
